# Optimizing a Trainium2 kernel written in Bass

```python
import numpy as np
import jax
import jax.numpy as jnp

def _softmax(x, axis=-1):
    return jax.nn.softmax(x, axis=axis)

def _gelu(x):
    return jax.nn.gelu(x, approximate=True)

def _silu(x):
    return jax.nn.silu(x)

def _sigmoid(x):
    return jax.nn.sigmoid(x)

def _layernorm(x, axis=-1, eps=1e-05):
    m = jnp.mean(x, axis=axis, keepdims=True)
    v = jnp.var(x, axis=axis, keepdims=True)
    return (x - m) / jnp.sqrt(v + eps)

def _scatter_add(tgt, idx, src, axis=0):
    return tgt.at[idx].add(src)

def _segment_sum(src, seg, n):
    return jax.ops.segment_sum(src, seg, n)
kernel_name = 'mk_gnn_preln_d2_gnn_r8_68b14b'

def setup_inputs(seed: int=0):
    np.random.seed(seed)
    _w = jnp.asarray

    def _rec_inputs():
        import jax
        import jax.numpy as jnp
        _gk = jax.random.key(seed)
        x = -0.000202 + 1 * jax.random.normal(jax.random.fold_in(_gk, 1), (6250, 128), jnp.float32)
        _s = jax.random.randint(jax.random.fold_in(_gk, 2), (100000,), 0, 6250, jnp.int32)
        _d = jax.random.randint(jax.random.fold_in(_gk, 3), (100000,), 0, 6250, jnp.int32)
        _loop = jnp.arange(6250, dtype=jnp.int32)
        src = jnp.concatenate([_s, _d, _loop])
        dst = jnp.concatenate([_d, _s, _loop])
        _o = jnp.argsort(dst, stable=True)
        src = src[_o]
        dst = dst[_o]
        edge_attr_64 = 0.000189758 + 1.00013 * jax.random.normal(jax.random.fold_in(_gk, 11), (206250, 64), jnp.float32)
        return (x, src, dst, edge_attr_64)
    x, src, dst, edge_attr_64 = _rec_inputs()

    def _L0_gnn_setup():
        import jax, jax.numpy as jnp
        import numpy as np
        N_NODES = 6250
        N_EDGES = 100000
        C = 128
        D = 64
        Z_DIM = 2 * C + D
        EPS = 1e-05
        key = jax.random.key(seed)
        ks = jax.random.split(key, 8)
        x = jax.random.normal(ks[0], (N_NODES, C), dtype=jnp.float32)
        edge_index = jax.random.randint(ks[1], (2, N_EDGES), 0, N_NODES, dtype=jnp.int64)
        edge_attr = jax.random.normal(ks[2], (N_EDGES, D), dtype=jnp.float32)
        scale = 1.0 / np.sqrt(Z_DIM)
        W_f = jax.random.normal(ks[3], (C, Z_DIM), dtype=jnp.float32) * scale
        b_f = jnp.zeros((C,), dtype=jnp.float32)
        W_s = jax.random.normal(ks[4], (C, Z_DIM), dtype=jnp.float32) * scale
        b_s = jnp.zeros((C,), dtype=jnp.float32)
        gamma = jnp.ones((C,), dtype=jnp.float32)
        beta = jnp.zeros((C,), dtype=jnp.float32)
        return {'x': x, 'edge_index': edge_index, 'edge_attr': edge_attr, 'W_f': W_f, 'b_f': b_f, 'W_s': W_s, 'b_s': b_s, 'gamma': gamma, 'beta': beta}
    _L0_gnn_all = _L0_gnn_setup()
    _L0_gnn_in = {k: v for k, v in _L0_gnn_all.items() if k in ('W_f', 'b_f', 'W_s', 'b_s', 'gamma', 'beta')}
    del _L0_gnn_all

    def _L1_gnn_setup():
        import jax, jax.numpy as jnp
        import numpy as np
        N_NODES = 12500
        N_EDGES = 200000
        IN_DIM = 128
        OUT_DIM = 128
        key = jax.random.key(seed)
        k1, k2, k3, k4 = jax.random.split(key, 4)
        x = jax.random.normal(k1, (N_NODES, IN_DIM), dtype=jnp.float32)
        edge_index = jax.random.randint(k2, (2, N_EDGES), 0, N_NODES, dtype=jnp.int32)
        W = jax.random.normal(k3, (IN_DIM, OUT_DIM), dtype=jnp.float32) / np.sqrt(IN_DIM)
        b = jax.random.normal(k4, (OUT_DIM,), dtype=jnp.float32) * 0.01
        return {'x': x, 'edge_index': edge_index, 'W': W, 'b': b}
    _L1_gnn_all = _L1_gnn_setup()
    _L1_gnn_in = {k: v for k, v in _L1_gnn_all.items() if k in ('W', 'b')}
    del _L1_gnn_all
    return {'x': x, 'src': src, 'dst': dst, 'edge_attr_64': edge_attr_64, 'L0_gnn_W_f': _L0_gnn_in['W_f'], 'L0_gnn_b_f': _L0_gnn_in['b_f'], 'L0_gnn_W_s': _L0_gnn_in['W_s'], 'L0_gnn_b_s': _L0_gnn_in['b_s'], 'L0_gnn_gamma': _L0_gnn_in['gamma'], 'L0_gnn_beta': _L0_gnn_in['beta'], 'L1_gnn_W': _L1_gnn_in['W'], 'L1_gnn_b': _L1_gnn_in['b']}

def reference(x, src, dst, edge_attr_64, L0_gnn_W_f, L0_gnn_b_f, L0_gnn_W_s, L0_gnn_b_s, L0_gnn_gamma, L0_gnn_beta, L1_gnn_W, L1_gnn_b):
    import jax
    import jax.numpy as jnp

    def _L0_gnn_ref(x, edge_index, edge_attr, W_f, b_f, W_s, b_s, gamma, beta):
        import jax, jax.numpy as jnp
        import numpy as np
        N_NODES = 6250
        N_EDGES = 100000
        C = 128
        D = 64
        Z_DIM = 2 * C + D
        EPS = 1e-05
        src = edge_index[0]
        dst = edge_index[1]
        z = jnp.concatenate([x[dst], x[src], edge_attr], axis=-1)
        gate = jax.nn.sigmoid(z @ W_f.T + b_f)
        val = jax.nn.softplus(z @ W_s.T + b_s)
        msg = gate * val
        summed = jax.ops.segment_sum(msg, dst, num_segments=N_NODES)
        count = jax.ops.segment_sum(jnp.ones((msg.shape[0],), msg.dtype), dst, num_segments=N_NODES)
        mean_agg = summed / jnp.maximum(count, 1.0)[:, None]
        out = x + mean_agg
        mu = jnp.mean(out, axis=0)
        var = jnp.mean((out - mu) ** 2, axis=0)
        y = gamma * (out - mu) * jax.lax.rsqrt(var + EPS) + beta
        return y

    def _L1_gnn_ref(x, edge_index, W, b):
        import jax, jax.numpy as jnp
        import numpy as np
        N_NODES = 12500
        N_EDGES = 200000
        IN_DIM = 128
        OUT_DIM = 128
        N = x.shape[0]
        row, col = (edge_index[0], edge_index[1])
        deg = jax.ops.segment_sum(jnp.ones(row.shape, x.dtype), col, num_segments=N)
        deg_inv_sqrt = jnp.where(deg > 0, jax.lax.rsqrt(deg), jnp.zeros_like(deg))
        norm = deg_inv_sqrt[row] * deg_inv_sqrt[col]
        agg = jax.ops.segment_sum(norm[:, None] * x[row], col, num_segments=N)
        out = jax.nn.relu(agg @ W + b)
        return out
    edge_index = jnp.stack([src, dst])
    h = jnp.maximum(_layernorm(x, axis=-1), 0.0)
    x = x + _L0_gnn_ref(h, edge_index, edge_attr_64, L0_gnn_W_f, L0_gnn_b_f, L0_gnn_W_s, L0_gnn_b_s, L0_gnn_gamma, L0_gnn_beta)
    h = jnp.maximum(_layernorm(x, axis=-1), 0.0)
    x = x + _L1_gnn_ref(h, edge_index, L1_gnn_W, L1_gnn_b)
    return x

_drawn_inputs = setup_inputs


def setup_inputs(seed=0):
    import zlib

    import numpy as np

    out = dict(_drawn_inputs(seed))
    spreads = {'L0_gnn_b_f': (0.0, 0.8),
     'L0_gnn_b_s': (0.0, 0.8),
     'L0_gnn_gamma': (1.0, 0.2),
     'L0_gnn_beta': (0.0, 0.1)}
    factors = {'L1_gnn_b': 8.0}
    for name, (base, spread) in spreads.items():
        noise = np.random.default_rng([zlib.crc32(name.encode()), seed]).standard_normal(out[name].shape)
        drawn = base * np.exp(spread * noise) if base else spread * noise
        out[name] = jnp.asarray(drawn.astype(out[name].dtype))
    for name, factor in factors.items():
        out[name] = (out[name] * factor).astype(out[name].dtype)
    return out
```

```python
import concourse.bass as bass
from concourse import mybir
from contextlib import ExitStack

N = 6250
C = 128
D = 64
E = 206250
P = 128
NB = 50
NP = NB * P
TPG = 4
GE = TPG * P
SLOTS = 4
G = -(-E // (GE * SLOTS)) * SLOTS
ITERS = G // SLOTS
TILES = G * TPG
W = 64
AW = C + 1
EPS = 1e-5
EXP_LN = "natural_log_exp_and_others"
STEP_CEN, STEP_VAR, STEP_H = 3, 5, 12
STEP_DEG, STEP_SUM, STEP_BN_CEN, STEP_SQ, STEP_BN_VAR = 14, 20, 25, 26, 27
STEP_CEN2, STEP_VAR2, STEP_T = 34, 36, 39
STEP_ACT_SQ2 = 6


def program(nc, x, src, dst_cols, dst_row, dst_first, edge_t, wf_t, ws_t, bf, bs, gamma, beta, w1, b1, out):
    f32, i32, bf16 = mybir.dt.float32, mybir.dt.int32, mybir.dt.bfloat16
    ALU, ACT, AX = mybir.AluOpType, mybir.ActivationFunctionType, mybir.AxisListType

    table_dst = nc.dram_tensor("table_dst", (NP, 2 * C), f32).ap()
    table_src = nc.dram_tensor("table_src", (NP, 2 * C), f32).ap()
    table_gcn = nc.dram_tensor("table_gcn", (NP, C), f32).ap()
    acc_rows = [nc.dram_tensor(f"acc_rows{i}", (NP, AW), f32).ap() for i in range(2)]

    x_v = x.rearrange("(b p) c -> p b c", p=P)
    gcn_v = table_gcn.rearrange("(b p) c -> p b c", p=P)

    ctx = ExitStack()
    with ctx:
        def sb(name, shape, dt=f32):
            return ctx.enter_context(nc.sbuf_tensor(name, shape, dt))

        def sem(name):
            return ctx.enter_context(nc.semaphore(name))

        def sems(name, n):
            return [sem(f"{name}{i}") for i in range(n)]

        x_rows = sb("x_rows", [P, NB, C])
        h_rows = sb("h_rows", [P, NB, C])
        acc = sb("acc", [P, 2, NP])
        scratch = acc[:, 0, :].rearrange("p (b c) -> p b c", c=C)
        dst_i = sb("dst_i", [P, TILES], i32)
        dst_rel = sb("dst_rel", [P, TILES])
        first_i = sb("first_i", [P, G], i32)
        first_f = sb("first_f", [P, G])
        ident = sb("ident", [P, P])
        iota_w = sb("iota_w", [P, W])
        iota_p = sb("iota_p", [P, 1])
        row_id = sb("row_id", [P, 1])
        ones_bf = sb("ones_bf", [P, P], bf16)
        inv_n = sb("inv_n", [P, P])
        avg = sb("avg", [P, 1])
        ones = sb("ones", [P, 1])
        below = sb("below", [P, P])
        w_nodes = sb("w_nodes", [P, 4 * C])
        w_edge = sb("w_edge", [D, 2 * C])
        bias = sb("bias", [P, 2 * C])
        gamma_b = sb("gamma_b", [P, C])
        beta_b = sb("beta_b", [P, C])
        w1_s = sb("w1_s", [P, C])
        b1_b = sb("b1_b", [P, C])
        stat = sb("stat", [P, 8, NB])
        chan = sb("chan", [P, 4, C])
        flag_c = sb("flag_c", [P, 4])
        flag_i = sb("flag_i", [1, 1], i32)
        slot_a = sb("slot_a", [P, 2, C])
        slot_b = sb("slot_b", [P, 2, C])
        slot_o = sb("slot_o", [P, 2, 4 * C])
        src_i = sb("src_i", [P, SLOTS, TPG], i32)
        got = sb("got", [P, SLOTS, TPG, 2 * C])
        lhs = sb("lhs", [P, SLOTS, GE])
        rhs = sb("rhs", [P, SLOTS, 2 * C])
        dst_b = sb("dst_b", [P, SLOTS, GE], i32)
        hot = sb("hot", [P, 2, TPG, W])
        pre = sb("pre", [P, 2, 2, 2 * C])
        uv = sb("uv", [P, 2, TPG, 2 * C])
        msg = sb("msg", [P, 2, TPG, C])
        bank = [ctx.enter_context(nc.psum_tensor(f"bank{i}", [P, 512], f32)) for i in range(8)]

        x_in, consts_in, index_in, pool_consts = sem("x_in"), sem("consts_in"), sem("index_in"), sem("pool_consts")
        weights_ready, flag_ok, flag_sum, flag_ready = sem("weights_ready"), sem("flag_ok"), sem("flag_sum"), sem("flag_ready")
        dve_step, act_step, pe_step = sem("dve_step"), sem("act_step"), sem("pe_step")
        acc_zero, acc_zero1 = sem("acc_zero"), sem("acc_zero1")
        t_copied, t_turned, t_slot, t_made, t_dst, t_src = (sem(n) for n in (
            "t_copied", "t_turned", "t_slot", "t_made", "t_dst", "t_src"))
        t_stored = sems("t_stored", 2)
        edge_in, srcs_in, rows_in = sems("edge_in", SLOTS), sems("srcs_in", SLOTS), sems("rows_in", SLOTS)
        onehot_t, pre_b, pre_a, added, act_done, fin, val_a, hot_ready, summed, accd = (sem(n) for n in (
            "onehot_t", "pre_b", "pre_a", "added", "act_done", "fin", "val_ready", "hot_ready", "summed", "accumulated"))
        act_chain = sem("act_chain")
        edges_done = sems("edges_done", 2)
        n_slot, n_prod, n_used, n_slot2, n_prod2, n_used2 = (sem(n) for n in (
            "n_slot", "n_prod", "n_used", "n_slot2", "n_prod2", "n_used2"))
        gcn_stored = sem("gcn_stored")
        srcs1_in, rows1_in = sems("srcs1_in", SLOTS), sems("rows1_in", SLOTS)
        hot1_ready, summed1, accd1 = sem("hot1_ready"), sem("summed1"), sem("accumulated1")
        f_slot, f_prod, f_bias, f_out = sem("f_slot"), sem("f_prod"), sem("f_bias"), sem("f_out")
        out_stored = sems("out_stored", 2)
        beta_added, waits_taken = sem("beta_added"), sem("waits_taken")
        g_in, g_rows, g_pre, g_half, g_add, g_actc, g_act, g_msg, g_sum, g_index, g_out, g_scat, g_dve, g_one = (
            sems(n, 2) for n in ("g_in", "g_rows", "g_pre", "g_half", "g_add", "g_actc", "g_act", "g_msg", "g_sum",
                                 "g_index", "g_out", "g_scat", "g_dve", "g_one"))
        g_back, g_turned, g_turn, g_zeroed = (sems(n, 2) for n in ("g_back", "g_turned", "g_turn", "g_zeroed"))

        block = ctx.enter_context(nc.Block())

        def blocks2(eng, step):
            for j in range(2):
                step(j, j)
            with eng.Fori(1, NB // 2) as i:
                for j in range(2):
                    step(i * 2 + j, j)

        def groups(eng, stages, before=None):
            def body(i):
                regs = before(i) if before else None
                for s in range(SLOTS):
                    for stage, lag in stages:
                        turn, at = (i, s - lag) if s >= lag else (i - 1, s - lag + SLOTS)
                        if isinstance(turn, int) and turn < 0:
                            continue
                        stage(turn * SLOTS + at, at, turn, regs and regs[s])
            body(0)
            with eng.Fori(1, ITERS) as i:
                body(i)
            most = max(lag for _, lag in stages)
            regs = before(ITERS) if before and most else None
            for d in range(most):
                for stage, lag in stages:
                    if d < lag:
                        g = G + d - lag
                        stage(g, g % SLOTS, ITERS - 1, regs and regs[d])

        def firsts(engine, lag):
            def load(i):
                at = i * SLOTS - lag
                skip = max(0, -at) if isinstance(i, int) else 0
                n = min(SLOTS, G - at) if isinstance(i, int) else SLOTS
                _, regs = nc.values_load_multi_w_load_instructions(
                    first_i[0:1, bass.ds(at + skip, n - skip)], engines=(engine,), min_val=0, max_val=N,
                    skip_runtime_bounds_check_because="a dst is a node, or N for the padding")
                return [None] * skip + list(regs)
            return load

        def late(g, n):
            return not isinstance(g, int) or g >= n

        def take_waits(eng):
            eng.sem_inc(waits_taken, 1)

        def sorted_enough(eng):
            eng.wait_ge(flag_ready, 1)
            return eng.value_load(flag_i[0:1, 0:1], min_val=0, max_val=P)

        def tiles(eng, step):
            for j in range(TPG):
                step(0, j, j)
            with eng.Fori(1, G) as g:
                for j in range(TPG):
                    step(g, j, g * TPG + j)

        g_same = hot[:, 0, :, :].rearrange("p t w -> p (t w)")[:, 0:P]
        g_before = hot[:, 1, :, :].rearrange("p t w -> p (t w)")[:, 0:P]
        g_msg_rows = uv[:, 1, 0, 0:AW]
        g_sum_rows = uv[:, 1, 1, 0:AW]
        g_uv = uv[:, 0, 0, :]
        g_col = flag_c
        g_dst, g_src, g_to = src_i[:, 1, 0:1], src_i[:, 0, 0:1], src_i[:, 2, 0:1]
        loads = (4, 3)

        def general_sync(sp, layer):
            sp.wait_ge((acc_zero, acc_zero1)[layer], 1)
            sp.dma_start(acc_rows[layer].rearrange("(b p) a -> p b a", p=P),
                         acc[:, 0, 0:AW].unsqueeze(1).to_broadcast([P, NB, AW])).then_inc(g_zeroed[layer], 16)
            sp.wait_ge(g_zeroed[layer], 16)

            def load(g, j, t):
                at = sp.snap(t) if not isinstance(t, int) else t
                if late(t, 1):
                    sp.wait_ge(g_scat[layer], t * 16)
                    take_waits(sp)
                sp.dma_start(g_src, src[bass.ds(g, 1), :, j:j + 1].rearrange("a p t -> (a p) t"),
                             allow_slow_non_contiguous=True).then_inc(g_in[layer], 16)
                sp.dma_start(g_dst, dst_cols[:, bass.ds(at, 1)], allow_slow_non_contiguous=True).then_inc(g_in[layer], 16)
                sp.dma_start(dst_b[:, 0, 0:P], dst_row[bass.ds(g, 1), j * P:(j + 1) * P].rearrange("a e -> (a e)")
                             .partition_broadcast(P)).then_inc(g_in[layer], 16)
                if layer == 0:
                    sp.dma_start(lhs[0:D, 0, 0:P], edge_t[bass.ds(g, 1), :, j * P:(j + 1) * P]
                                 .rearrange("a k e -> (a k) e")).then_inc(g_in[layer], 16)
            tiles(sp, load)
            sp.wait_ge(g_scat[layer], 16 * TILES)
            def back(b, j):
                rows = sp.snap(b * P) if not isinstance(b, int) else b * P
                if late(b, 1):
                    sp.wait_ge(g_turn[layer], b)
                take_waits(sp)
                sp.dma_start(slot_o[:, j, 0:AW], acc_rows[layer][bass.ds(rows, P), :]).then_inc(g_back[layer], 16)
            blocks2(sp, back)

        def general_pool(pool, layer):
            def move(g, j, t):
                pool.wait_ge(g_in[layer], (t + 1) * (16 * loads[layer]))
                take_waits(pool)
                if layer == 0:
                    pool.indirect_dma_start(out=got[:, 0, 0, :], out_offset=None, in_=table_dst,
                                            in_offset=bass.IndirectOffsetOnAxis(ap=g_dst, axis=0)).then_inc(g_rows[layer], 16)
                table, width = ((table_src, 2 * C), (table_gcn, C))[layer]
                pool.indirect_dma_start(out=got[:, 0, 1, 0:width], out_offset=None, in_=table,
                                        in_offset=bass.IndirectOffsetOnAxis(ap=g_src, axis=0)).then_inc(g_rows[layer], 16)
                pool.wait_ge(g_out[layer], t + 1)
                take_waits(pool)
                pool.indirect_dma_start(out=acc_rows[layer], out_offset=bass.IndirectOffsetOnAxis(ap=g_to, axis=0),
                                        in_=g_sum_rows, in_offset=None, compute_op=ALU.add).then_inc(g_scat[layer], 16)
            tiles(pool, move)

        def general_act(act, layer):
            if layer:
                return
            u, v = g_uv[:, 0:C], g_uv[:, C:2 * C]
            nc.scalar.preload_act_table_set(EXP_LN)
            def acts(g, j, t):
                act.wait_ge(g_add[0], t + 1)
                nc.scalar.activation(u, pre[:, 0, 1, 0:C], ACT.Exp).then_inc(g_actc[0], 1)
                nc.scalar.activation(v, pre[:, 0, 1, C:2 * C], ACT.Abs).then_inc(g_actc[0], 1)
                act.wait_ge(g_actc[0], t * 4 + 2)
                nc.scalar.activation(v, v, ACT.Exp, scale=-1.0).then_inc(g_actc[0], 1)
                act.wait_ge(g_actc[0], t * 4 + 3)
                nc.scalar.activation(g_uv, g_uv, ACT.Ln, bias=1.0).then_inc(g_actc[0], 1)
                act.wait_ge(g_actc[0], t * 4 + 4)
                nc.scalar.activation(u, u, ACT.Exp, scale=-1.0).then_inc(g_act[0], 1)
            tiles(act, acts)

        def general_dve(dve, layer):
            n_links = (7, 6)[layer]
            link_sem = g_dve[layer]
            nc.vector.memset(g_msg_rows[:, C:AW], 1.0).then_inc(g_one[layer], 1)
            nc.vector.tensor_scalar(g_col[:, 3:4], row_id[:, :], float(N + 1), None, ALU.add).then_inc(g_one[layer], 1)
            dve.wait_ge(g_one[layer], 2)

            def work(g, j, t):
                made = [0]

                def link(ins):
                    made[0] += 1
                    ins.then_inc(link_sem, 1)
                    dve.wait_ge(link_sem, t * n_links + made[0])

                dve.wait_ge(g_in[layer], (t + 1) * (16 * loads[layer]))
                link(nc.vector.tensor_copy(g_col[:, 0:1], g_dst))
                link(nc.vector.tensor_scalar(g_same, dst_b[:, 0, 0:P], g_col[:, 0:1], None, ALU.is_equal))
                link(nc.vector.tensor_tensor(g_before, g_same, below[:, :], ALU.mult))
                link(nc.vector.tensor_reduce(g_col[:, 1:2], g_before, AX.X, ALU.add))
                link(nc.vector.tensor_scalar(g_col[:, 2:3], g_col[:, 1:2], 0.0, None, ALU.is_equal))
                link(nc.vector.tensor_scalar(g_col[:, 1:2], g_col[:, 0:1], g_col[:, 3:4], g_col[:, 2:3],
                                             ALU.subtract, ALU.mult))
                nc.vector.tensor_tensor(g_to, g_col[:, 1:2], g_col[:, 3:4], ALU.add).then_inc(g_index[layer], 1)
                dve.wait_ge(g_rows[layer], (t + 1) * (32, 16)[layer])
                if layer == 0:
                    dve.wait_ge(g_pre[0], t + 1)
                    nc.vector.tensor_tensor(pre[:, 0, 0, :], bank[2][:, 0:2 * C], got[:, 0, 0, :], ALU.add
                                            ).then_inc(g_half[0], 1)
                    dve.wait_ge(g_half[0], t + 1)
                    nc.vector.tensor_tensor(pre[:, 0, 1, :], pre[:, 0, 0, :], got[:, 0, 1, :], ALU.add
                                            ).then_inc(g_add[0], 1)
                    dve.wait_ge(g_act[0], t + 1)
                    link(nc.vector.scalar_tensor_tensor(out=g_uv[:, C:2 * C], in0=pre[:, 0, 1, C:2 * C], scalar=0.0,
                                                        in1=g_uv[:, C:2 * C], op0=ALU.max, op1=ALU.add))
                    nc.vector.tensor_tensor(g_msg_rows[:, 0:C], g_uv[:, C:2 * C], g_uv[:, 0:C], ALU.mult
                                            ).then_inc(g_msg[0], 1)
                else:
                    nc.vector.tensor_copy(g_msg_rows[:, 0:C], got[:, 0, 1, 0:C]).then_inc(g_msg[1], 1)
                assert made[0] == n_links
                dve.wait_ge(g_sum[layer], t + 1)
                dve.wait_ge(g_index[layer], t + 1)
                nc.vector.tensor_copy(g_sum_rows, bank[4][:, 0:AW]).then_inc(g_out[layer], 1)
            tiles(dve, work)
            def back(b, j):
                dve.wait_ge(g_turned[layer], b + 1)
                nc.vector.tensor_copy(acc[:, :, bass.ds(b * P, P)], bank[j][:, 0:2 * P].rearrange("p (a n) -> p a n", a=2)
                                      ).then_inc(g_turn[layer], 1)
            blocks2(dve, back)
            dve.wait_ge(g_turn[layer], NB)

        def general_pe(pe, layer):
            def work(g, j, t):
                if layer == 0:
                    pe.wait_ge(g_in[0], (t + 1) * (16 * loads[0]))
                    nc.tensor.matmul(bank[2][:, 0:2 * C], lhs[0:D, 0, 0:P], rhs[0:D, 0, :], start=True, stop=True
                                     ).then_inc(g_pre[0], 1)
                pe.wait_ge(g_msg[layer], t + 1)
                nc.tensor.matmul(bank[4][:, 0:AW], g_same, g_msg_rows, start=True, stop=True).then_inc(g_sum[layer], 1)
            tiles(pe, work)
            def back(b, j):
                pe.wait_ge(g_back[layer], (b + 1) * 16)
                if late(b, 2):
                    pe.wait_ge(g_turn[layer], b - 1)
                nc.tensor.transpose(bank[j][:, 0:P], slot_o[:, j, 0:C], ident[:, :])
                nc.tensor.matmul(bank[j][:, P:2 * P], slot_o[:, j, C:AW].to_broadcast([P, P]), ident[:, :],
                                 start=True, stop=True).then_inc(g_turned[layer], 1)
            blocks2(pe, back)

        @block.sync
        def _(sp):
            sp.dma_start(x_rows[:, :, :], x_v).then_inc(x_in, 16)
            sp.dma_start(dst_i[:, :], dst_cols).then_inc(index_in, 16)
            sp.dma_start(first_i[:, :], dst_first.partition_broadcast(P)).then_inc(index_in, 16)
            for k, part in enumerate((wf_t[0:C], ws_t[0:C], wf_t[C:2 * C], ws_t[C:2 * C])):
                sp.dma_start(w_nodes[:, k * C:(k + 1) * C], part).then_inc(consts_in, 16)
            sp.dma_start(w_edge[:, 0:C], wf_t[2 * C:2 * C + D]).then_inc(consts_in, 16)
            sp.dma_start(w_edge[:, C:2 * C], ws_t[2 * C:2 * C + D]).then_inc(consts_in, 16)
            for tile, row in ((bias[:, 0:C], bf), (bias[:, C:2 * C], bs), (gamma_b[:, :], gamma),
                              (beta_b[:, :], beta), (b1_b[:, :], b1)):
                sp.dma_start(tile, row.partition_broadcast(P)).then_inc(consts_in, 16)
            sp.dma_start(w1_s[:, :], w1).then_inc(consts_in, 16)

            def store_tables(b, j):
                rows = sp.snap(b * P) if not isinstance(b, int) else b * P
                n = b + 1
                sp.wait_ge(t_dst, n)
                sp.wait_ge(t_src, n)
                sp.dma_start(table_dst[bass.ds(rows, P), :], slot_o[:, j, 0:2 * C]).then_inc(t_stored[j], 16)
                sp.dma_start(table_src[bass.ds(rows, P), :], slot_o[:, j, 2 * C:4 * C]).then_inc(t_stored[j], 16)
            blocks2(sp, store_tables)
            for j in range(2):
                sp.wait_ge(t_stored[j], 16 * NB)

            def fast0():
                def load_edges(g, s, i, first):
                    if late(g, SLOTS):
                        sp.wait_ge(pre_a, g - SLOTS + 1)
                    sp.dma_start(lhs[0:D, s, :], edge_t[bass.ds(g, 1)].rearrange("a k e -> (a k) e")).then_inc(edge_in[s], 16)
                    sp.dma_start(dst_b[D:P, s, :], dst_row[bass.ds(g, 1), :].rearrange("a e -> (a e)")
                                 .partition_broadcast(W)).then_inc(edge_in[s], 16)
                    sp.dma_start(rhs[D:P, s, :], table_dst[bass.ds(first, W), :]).then_inc(edge_in[s], 16)
                    if late(g, SLOTS):
                        sp.wait_ge(rows_in[s], i * (16 * TPG))
                    sp.dma_start(src_i[:, s, :], src[bass.ds(g, 1)].rearrange("a p t -> (a p) t")).then_inc(srcs_in[s], 16)
                groups(sp, [(load_edges, 0)], firsts(mybir.EngineType.SP, 0))

            def fast1():
                def load_srcs(g, s, i, _):
                    if late(g, SLOTS):
                        sp.wait_ge(rows1_in[s], i * (16 * TPG))
                    sp.dma_start(src_i[:, s, :], src[bass.ds(g, 1)].rearrange("a p t -> (a p) t")).then_inc(srcs1_in[s], 16)
                groups(sp, [(load_srcs, 0)])

            verdict = sorted_enough(sp)
            with sp.If(verdict == P):
                fast0()
            with sp.Else():
                general_sync(sp, 0)
            sp.wait_ge(dve_step, STEP_T)
            sp.dma_start(gcn_v, h_rows[:, :, :]).then_inc(gcn_stored, 16)
            sp.wait_ge(gcn_stored, 16)
            with sp.If(verdict == P):
                fast1()
            with sp.Else():
                general_sync(sp, 1)

            def store_out(b, j):
                rows = sp.snap(b * P) if not isinstance(b, int) else b * P
                sp.wait_ge(f_out, b + 1)
                sp.dma_start(out[bass.ds(rows, P), :], slot_o[:, j, C:2 * C]).then_inc(out_stored[j], 16)
            blocks2(sp, store_out)
            for j in range(2):
                sp.wait_ge(out_stored[j], 16 * (NB // 2))

        @block.gpsimd
        def _(pool):
            nc.gpsimd.memset(ident[:, :], 0.0).then_inc(pool_consts, 1)
            nc.gpsimd.memset(below[:, :], 1.0).then_inc(pool_consts, 1)
            nc.gpsimd.memset(ones_bf[:, :], 1.0).then_inc(pool_consts, 1)
            nc.gpsimd.memset(inv_n[:, :], 1.0 / N).then_inc(pool_consts, 1)
            nc.gpsimd.memset(avg[:, :], 1.0 / P).then_inc(pool_consts, 1)
            nc.gpsimd.memset(ones[:, :], 1.0).then_inc(pool_consts, 1)
            nc.gpsimd.iota(iota_w[:, :], pattern=[[1, W]], base=0, channel_multiplier=0,
                           allow_small_or_imprecise_dtypes=True).then_inc(pool_consts, 1)
            nc.gpsimd.iota(iota_p[:, :], pattern=[[0, 1]], base=-(P - W), channel_multiplier=1,
                           allow_small_or_imprecise_dtypes=True).then_inc(pool_consts, 1)
            nc.gpsimd.iota(row_id[:, :], pattern=[[0, 1]], base=0, channel_multiplier=1,
                           allow_small_or_imprecise_dtypes=True).then_inc(pool_consts, 1)
            pool.wait_ge(pool_consts, 9)
            nc.gpsimd.affine_select(out=ident[:, :], in_=ident[:, :], compare_op=ALU.not_equal, fill=1.0, base=0,
                                    pattern=[[-1, P]], channel_multiplier=1).then_inc(pool_consts, 1)
            nc.gpsimd.affine_select(out=below[:, :], in_=below[:, :], compare_op=ALU.is_gt, fill=0.0, base=0,
                                    pattern=[[-1, P]], channel_multiplier=1).then_inc(pool_consts, 1)

            pool.wait_ge(dve_step, STEP_H)
            def copy_h(b, j):
                if late(b, 2):
                    pool.wait_ge(t_turned, b - 1)
                nc.gpsimd.tensor_copy(slot_a[:, j, :], h_rows[:, bass.ds(b, 1), :].rearrange("p a c -> p (a c)")
                                      ).then_inc(t_copied, 1)
            blocks2(pool, copy_h)
            pool.wait_ge(act_step, 1)
            pool.wait_ge(dve_step, STEP_VAR)
            nc.gpsimd.memset(acc[:, :, :], 0.0).then_inc(acc_zero, 1)
            for j in range(2):
                pool.wait_ge(t_stored[j], 16 * NB)

            def gathers(table, width, rows, srcs, used):
                def gather(g, s, i, _):
                    pool.wait_ge(srcs[s], (i + 1) * 16)
                    if late(g, SLOTS):
                        for done in used:
                            pool.wait_ge(done, g - SLOTS + 1)
                    take_waits(pool)
                    for t in range(TPG):
                        pool.indirect_dma_start(
                            out=got[:, s, t, 0:width], out_offset=None, in_=table,
                            in_offset=bass.IndirectOffsetOnAxis(ap=src_i[:, s, t:t + 1], axis=0)).then_inc(rows[s], 16)
                groups(pool, [(gather, 0)])

            verdict = sorted_enough(pool)
            with pool.If(verdict == P):
                gathers(table_src, 2 * C, rows_in, srcs_in, (pre_a, added))
            with pool.Else():
                general_pool(pool, 0)
            pool.wait_ge(edges_done[0], 1)
            pool.wait_ge(consts_in, 16 * 12)
            nc.gpsimd.tensor_tensor(x_rows[:, :, :], x_rows[:, :, :],
                                    beta_b[:, :].unsqueeze(1).to_broadcast([P, NB, C]), ALU.add).then_inc(beta_added, 1)
            pool.wait_ge(act_step, STEP_ACT_SQ2)
            pool.wait_ge(dve_step, STEP_T)
            nc.gpsimd.memset(acc[:, 0, :], 0.0).then_inc(acc_zero1, 1)
            pool.wait_ge(gcn_stored, 16)
            with pool.If(verdict == P):
                gathers(table_gcn, C, rows1_in, srcs1_in, (summed1,))
            with pool.Else():
                general_pool(pool, 1)

        @block.scalar
        def _(act):
            act.wait_ge(consts_in, 16 * 12)
            for part in (w_nodes[:, 0:C], w_nodes[:, 2 * C:3 * C], bias[:, 0:C]):
                nc.scalar.mul(part, part, -1.0).then_inc(weights_ready, 1)
            for s in range(SLOTS):
                nc.scalar.mul(rhs[0:D, s, 0:C], w_edge[:, 0:C], -1.0).then_inc(weights_ready, 1)
                nc.scalar.copy(rhs[0:D, s, C:2 * C], w_edge[:, C:2 * C]).then_inc(weights_ready, 1)

            def square(step, count):
                act.wait_ge(dve_step, step)
                nc.scalar.activation(scratch, h_rows[:, :, :], ACT.Square).then_inc(act_step, 1)

            def root(step, ap):
                act.wait_ge(dve_step, step)
                nc.scalar.activation(ap, ap, ACT.Sqrt).then_inc(act_step, 1)

            square(STEP_CEN, 1)
            root(STEP_VAR, stat[:, 2, :])

            def tables(b, j):
                act.wait_ge(t_turned, b + 1)
                if late(b, 2):
                    act.wait_ge(t_made, b - 1)
                nc.scalar.copy(slot_b[:, j, :], bank[j][:, 0:C]).then_inc(t_slot, 1)
                act.wait_ge(t_made, b + 1)
                if late(b, 2):
                    act.wait_ge(t_stored[j], (b - j) * 16)
                nc.scalar.copy(slot_o[:, j, 2 * C:4 * C], bank[4 + j][:, 0:2 * C]).then_inc(t_src, 1)
            blocks2(act, tables)

            def fast0():
                nc.scalar.preload_act_table_set(EXP_LN)
                def acts(g, s, i, _):
                    k = s % 2
                    u, v = uv[:, k, :, 0:C], uv[:, k, :, C:2 * C]
                    act.wait_ge(added, g + 1)
                    if late(g, 2):
                        act.wait_ge(fin, g - 1)
                    nc.scalar.activation(u[:, 2:4, :], pre[:, k, :, 0:C], ACT.Exp).then_inc(act_chain, 1)
                    nc.scalar.activation(v[:, 2:4, :], pre[:, k, :, C:2 * C], ACT.Abs).then_inc(act_chain, 1)
                    act.wait_ge(pre_a, g + 1)
                    pa = bank[k][:, :].rearrange("p (t c) -> p t c", t=2)
                    nc.scalar.activation(u[:, 0:2, :], pa[:, :, 0:C], ACT.Exp).then_inc(act_chain, 1)
                    nc.scalar.activation(v[:, 0:2, :], pa[:, :, C:2 * C], ACT.Abs).then_inc(act_chain, 1)
                    act.wait_ge(act_chain, g * 6 + 4)
                    nc.scalar.activation(v, v, ACT.Exp, scale=-1.0).then_inc(act_chain, 1)
                    act.wait_ge(act_chain, g * 6 + 5)
                    nc.scalar.activation(uv[:, k, :, :], uv[:, k, :, :], ACT.Ln, bias=1.0).then_inc(act_chain, 1)
                    act.wait_ge(act_chain, g * 6 + 6)
                    nc.scalar.activation(u, u, ACT.Exp, scale=-1.0).then_inc(act_done, 1)
                groups(act, [(acts, 0)])

            verdict = sorted_enough(act)
            with act.If(verdict == P):
                fast0()
            with act.Else():
                general_act(act, 0)

            act.wait_ge(edges_done[0], 1)
            def count_block(b, j):
                if late(b, 2):
                    act.wait_ge(n_prod, b - 1)
                nc.scalar.copy(slot_b[:, j, :], acc[:, 1, bass.ds(b * P, P)]).then_inc(n_slot, 1)
            blocks2(act, count_block)
            def sum_block(b, j):
                if late(b, 2):
                    act.wait_ge(n_prod2, b - 1)
                nc.scalar.copy(slot_a[:, j, :], acc[:, 0, bass.ds(b * P, P)]).then_inc(n_slot2, 1)
            blocks2(act, sum_block)
            root(STEP_DEG, stat[:, 4, :])
            square(STEP_BN_CEN, 4)
            root(STEP_BN_VAR, chan[:, 1, :])
            square(STEP_CEN2, 6)
            root(STEP_VAR2, stat[:, 6, :])

            act.wait_ge(edges_done[1], 1)
            def final_block(b, j):
                if late(b, 2):
                    act.wait_ge(f_prod, b - 1)
                nc.scalar.copy(slot_a[:, j, :], acc[:, 0, bass.ds(b * P, P)]).then_inc(f_slot, 1)
            blocks2(act, final_block)

        @block.vector
        def _(dve):
            steps = [0]

            def link(ins):
                steps[0] += 1
                ins.then_inc(dve_step, 1)
                dve.wait_ge(dve_step, steps[0])
                return steps[0]

            def rows_b(col):
                return col.unsqueeze(2).to_broadcast([P, NB, C])

            def cols_b(row):
                return row.unsqueeze(1).to_broadcast([P, NB, C])

            def layer_norm(cen, var, sq):
                link(nc.vector.tensor_reduce(stat[:, 0, :], x_rows[:, :, :], AX.X, ALU.add))
                link(nc.vector.tensor_scalar(stat[:, 1, :], stat[:, 0, :], 1.0 / C, None, ALU.mult))
                assert link(nc.vector.tensor_tensor(h_rows[:, :, :], x_rows[:, :, :], rows_b(stat[:, 1, :]),
                                                    ALU.subtract)) == cen
                dve.wait_ge(act_step, sq)
                link(nc.vector.tensor_reduce(stat[:, 0, :], scratch, AX.X, ALU.add))

            dve.wait_ge(x_in, 16)
            layer_norm(STEP_CEN, STEP_VAR, 1)
            assert link(nc.vector.tensor_scalar(stat[:, 2, :], stat[:, 0, :], 1.0 / C, EPS, ALU.mult, ALU.add)) == STEP_VAR
            dve.wait_ge(index_in, 32)
            link(nc.vector.tensor_copy(first_f[:, :], first_i[:, :]))
            rel = dst_rel[:, :].rearrange("p (g t) -> p g t", t=TPG)
            link(nc.vector.tensor_tensor(rel, dst_i[:, :].rearrange("p (g t) -> p g t", t=TPG),
                                         first_i[:, :].unsqueeze(2).to_broadcast([P, G, TPG]), ALU.subtract))
            link(nc.vector.tensor_reduce(flag_c[:, 0:1], dst_rel[:, :], AX.X, ALU.min))
            link(nc.vector.tensor_reduce(flag_c[:, 1:2], dst_rel[:, :], AX.X, ALU.max))
            link(nc.vector.tensor_scalar(flag_c[:, 2:3], flag_c[:, 0:1], 0.0, None, ALU.is_ge))
            nc.vector.scalar_tensor_tensor(out=flag_c[:, 3:4], in0=flag_c[:, 1:2], scalar=float(W - 1), in1=flag_c[:, 2:3],
                                           op0=ALU.is_le, op1=ALU.mult).then_inc(flag_ok, 1)
            dve.wait_ge(flag_sum, 1)
            nc.vector.tensor_copy(flag_i[0:1, 0:1], bank[7][0:1, 0:1]).then_inc(flag_ready, 1)
            dve.wait_ge(act_step, 2)
            link(nc.vector.reciprocal(stat[:, 3, :], stat[:, 2, :]))
            assert link(nc.vector.scalar_tensor_tensor(out=h_rows[:, :, :], in0=h_rows[:, :, :], scalar=0.0,
                                                       in1=rows_b(stat[:, 3, :]), op0=ALU.max, op1=ALU.mult)) == STEP_H

            dve.wait_ge(weights_ready, 3 + 2 * SLOTS)
            def tables(b, j):
                dve.wait_ge(t_made, b + 1)
                if late(b, 2):
                    dve.wait_ge(t_stored[j], (b - j) * 16)
                nc.vector.tensor_tensor(slot_o[:, j, 0:2 * C], bank[2 + j][:, 0:2 * C], bias[:, :], ALU.add
                                        ).then_inc(t_dst, 1)
            blocks2(dve, tables)
            dve.wait_ge(acc_zero, 1)
            for j in range(2):
                dve.wait_ge(t_stored[j], 16 * NB)

            def one_hot(g, k, ready, used):
                if late(g, 2):
                    dve.wait_ge(used, g - 1)
                nc.vector.tensor_tensor(
                    hot[:, k, :, :], iota_w[:, :].unsqueeze(1).to_broadcast([P, TPG, W]),
                    dst_rel[:, bass.ds(g * TPG, TPG)].unsqueeze(2).to_broadcast([P, TPG, W]), ALU.is_equal
                ).then_inc(ready, 1)

            def accumulate(g, k, first, parts, ready, done):
                dve.wait_ge(ready, g + 1)
                if late(g, 1):
                    dve.wait_ge(done, g)
                place = acc[:, 0:parts, bass.ds(first, W)]
                nc.vector.tensor_tensor(place, bank[4 + k][:, 0:parts * W].rearrange("p (a w) -> p a w", a=parts),
                                        place, ALU.add).then_inc(done, 1)

            def fast0():
                def onehot_turned(g, s, i, first):
                    dve.wait_ge(edge_in[s], (i + 1) * 48)
                    nc.vector.tensor_scalar(lhs[D:P, s, :], dst_b[D:P, s, :], first_f[D:P, bass.ds(g, 1)],
                                            iota_p[D:P, :], ALU.subtract, ALU.is_equal).then_inc(onehot_t, 1)

                def add(g, s, i, _):
                    k = s % 2
                    dve.wait_ge(pre_b, g + 1)
                    dve.wait_ge(rows_in[s], (i + 1) * (16 * TPG))
                    if late(g, 2):
                        dve.wait_ge(fin, g - 1)
                    nc.vector.tensor_tensor(pre[:, k, :, :], bank[2 + k][:, :].rearrange("p (t c) -> p t c", t=2),
                                            got[:, s, 2:4, :], ALU.add).then_inc(added, 1)

                def finish(g, s, i, _):
                    k = s % 2
                    u, v = uv[:, k, :, 0:C], uv[:, k, :, C:2 * C]
                    dve.wait_ge(act_done, g + 1)
                    nc.vector.scalar_tensor_tensor(out=v[:, 0:2, :], in0=bank[k][:, :].rearrange("p (t c) -> p t c", t=2)[:, :, C:2 * C],
                                                   scalar=0.0, in1=v[:, 0:2, :], op0=ALU.max, op1=ALU.add).then_inc(val_a, 1)
                    nc.vector.scalar_tensor_tensor(out=v[:, 2:4, :], in0=pre[:, k, :, C:2 * C],
                                                   scalar=0.0, in1=v[:, 2:4, :], op0=ALU.max, op1=ALU.add).then_inc(val_a, 1)
                    one_hot(g, k, hot_ready, summed)
                    dve.wait_ge(val_a, (g + 1) * 2)
                    nc.vector.tensor_tensor(msg[:, k, :, :], v, u, ALU.mult).then_inc(fin, 1)

                def acc_stage(g, s, i, first):
                    accumulate(g, s % 2, first, 2, summed, accd)
                groups(dve, [(onehot_turned, 0), (add, 1), (finish, 2), (acc_stage, 3)], firsts(mybir.EngineType.DVE, 3))

            def fast1():
                def hot_stage(g, s, i, _):
                    one_hot(g, s % 2, hot1_ready, summed1)

                def acc_stage(g, s, i, first):
                    accumulate(g, s % 2, first, 1, summed1, accd1)
                groups(dve, [(hot_stage, 0), (acc_stage, 1)], firsts(mybir.EngineType.DVE, 1))

            verdict = sorted_enough(dve)
            with dve.If(verdict == P):
                fast0()
                dve.wait_ge(accd, G)
            with dve.Else():
                general_dve(dve, 0)
            nc.vector.memset(acc[:, :, N:NP], 0.0).then_inc(edges_done[0], 1)

            dve.wait_ge(n_prod, NB)
            link(nc.vector.tensor_copy(stat[:, 5, :], bank[6][:, 0:NB]))
            assert link(nc.vector.tensor_scalar(stat[:, 4, :], stat[:, 5, :], 1.0, None, ALU.max)) == STEP_DEG
            link(nc.vector.tensor_scalar(stat[:, 7, :], stat[:, 5, :], 1.0, None, ALU.max))
            link(nc.vector.reciprocal(stat[:, 2, :], stat[:, 7, :]))
            link(nc.vector.tensor_scalar(stat[:, 3, :], stat[:, 5, :], 1.0, None, ALU.min))
            def mean_block(b, j):
                dve.wait_ge(n_prod2, b + 1)
                rows = h_rows[:, bass.ds(b, 1), :].rearrange("p a c -> p (a c)")
                nc.vector.scalar_tensor_tensor(out=rows, in0=bank[j][:, 0:C], scalar=stat[:, 2, bass.ds(b, 1)],
                                               in1=rows, op0=ALU.mult, op1=ALU.add).then_inc(n_used2, 1)
            blocks2(dve, mean_block)
            dve.wait_ge(n_used2, NB)
            dve.wait_ge(act_step, 3)
            link(nc.vector.reciprocal(stat[:, 5, :], stat[:, 4, :]))
            link(nc.vector.tensor_tensor(stat[:, 4, :], stat[:, 5, :], stat[:, 3, :], ALU.mult))

            by_chan = h_rows[:, :, :].rearrange("p b c -> p c b")
            assert link(nc.vector.tensor_reduce(chan[:, 0, :], by_chan, AX.X, ALU.add)) == STEP_SUM
            dve.wait_ge(pe_step, 1)
            link(nc.vector.tensor_copy(chan[:, 1, :], bank[7][:, 0:C]))
            link(nc.vector.tensor_tensor(h_rows[:, :, :], h_rows[:, :, :], cols_b(chan[:, 1, :]), ALU.subtract))
            link(nc.vector.tensor_scalar(flag_c[:, 0:1], row_id[:, :], float(N % P), None, ALU.is_lt))
            link(nc.vector.tensor_scalar(h_rows[:, N // P, :], h_rows[:, N // P, :], flag_c[:, 0:1], None, ALU.mult))
            assert link(nc.vector.memset(h_rows[:, N // P + 1:NB, :], 0.0)) == STEP_BN_CEN
            dve.wait_ge(act_step, 4)
            assert link(nc.vector.tensor_reduce(chan[:, 0, :], scratch.rearrange("p b c -> p c b"), AX.X, ALU.add)) == STEP_SQ
            dve.wait_ge(pe_step, 2)
            assert link(nc.vector.tensor_scalar(chan[:, 1, :], bank[7][:, 0:C], EPS, None, ALU.add)) == STEP_BN_VAR
            dve.wait_ge(act_step, 5)
            link(nc.vector.reciprocal(chan[:, 2, :], chan[:, 1, :]))
            link(nc.vector.tensor_tensor(chan[:, 3, :], chan[:, 2, :], gamma_b[:, :], ALU.mult))
            link(nc.vector.tensor_tensor(h_rows[:, :, :], h_rows[:, :, :], cols_b(chan[:, 3, :]), ALU.mult))
            dve.wait_ge(beta_added, 1)
            link(nc.vector.tensor_tensor(x_rows[:, :, :], x_rows[:, :, :], h_rows[:, :, :], ALU.add))

            layer_norm(STEP_CEN2, STEP_VAR2, STEP_ACT_SQ2)
            assert link(nc.vector.tensor_scalar(stat[:, 6, :], stat[:, 0, :], 1.0 / C, EPS, ALU.mult, ALU.add)) == STEP_VAR2
            dve.wait_ge(act_step, STEP_ACT_SQ2 + 1)
            link(nc.vector.reciprocal(stat[:, 0, :], stat[:, 6, :]))
            link(nc.vector.tensor_tensor(stat[:, 1, :], stat[:, 0, :], stat[:, 4, :], ALU.mult))
            assert link(nc.vector.scalar_tensor_tensor(out=h_rows[:, :, :], in0=h_rows[:, :, :], scalar=0.0,
                                                       in1=rows_b(stat[:, 1, :]), op0=ALU.max, op1=ALU.mult)) == STEP_T

            dve.wait_ge(acc_zero1, 1)
            with dve.If(verdict == P):
                fast1()
                dve.wait_ge(accd1, G)
            with dve.Else():
                general_dve(dve, 1)
            nc.vector.memset(acc[:, 0, N:NP], 0.0).then_inc(edges_done[1], 1)

            def final_pair(b0):
                for j in range(2):
                    b = b0 + j
                    dve.wait_ge(f_prod, b + 1)
                    if late(b, 2):
                        dve.wait_ge(out_stored[j], b0 * 8)
                    nc.vector.scalar_tensor_tensor(out=slot_o[:, j, 0:C], in0=bank[j][:, 0:C], scalar=stat[:, 4, bass.ds(b, 1)],
                                                   in1=b1_b[:, :], op0=ALU.mult, op1=ALU.add).then_inc(f_bias, 1)
                for j in range(2):
                    b = b0 + j
                    dve.wait_ge(f_bias, b + 1)
                    nc.vector.scalar_tensor_tensor(out=slot_o[:, j, C:2 * C], in0=slot_o[:, j, 0:C], scalar=0.0,
                                                   in1=x_rows[:, bass.ds(b, 1), :].rearrange("p a c -> p (a c)"),
                                                   op0=ALU.max, op1=ALU.add).then_inc(f_out, 1)
            final_pair(0)
            with dve.Fori(1, NB // 2) as i:
                final_pair(i * 2)

        @block.tensor
        def _(pe):
            pe.wait_ge(pool_consts, 11)
            pe.wait_ge(flag_ok, 1)
            nc.tensor.matmul(bank[7][0:1, 0:1], flag_c[:, 3:4], ones[:, :], start=True, stop=True).then_inc(flag_sum, 1)
            pe.wait_ge(weights_ready, 3 + 2 * SLOTS)

            def turn(b, j):
                pe.wait_ge(t_copied, b + 1)
                if late(b, 2):
                    pe.wait_ge(t_slot, b - 1)
                nc.tensor.transpose(bank[j][:, 0:C], slot_a[:, j, :], ident[:, :]).then_inc(t_turned, 1)
                pe.wait_ge(t_slot, b + 1)
                if late(b, 2):
                    pe.wait_ge(t_dst, b - 1)
                    pe.wait_ge(t_src, b - 1)
                nc.tensor.matmul(bank[2 + j][:, 0:2 * C], slot_b[:, j, :], w_nodes[:, 0:2 * C], start=True, stop=True)
                nc.tensor.matmul(bank[4 + j][:, 0:2 * C], slot_b[:, j, :], w_nodes[:, 2 * C:4 * C], start=True, stop=True
                                 ).then_inc(t_made, 1)
            blocks2(pe, turn)
            pe.wait_ge(t_dst, NB)
            pe.wait_ge(t_src, NB)

            def fast0():
                def products(g, s, i, _):
                    k = s % 2
                    pe.wait_ge(onehot_t, g + 1)
                    if late(g, 2):
                        pe.wait_ge(added, g - 1)
                    for t in (2, 3):
                        last = nc.tensor.matmul(bank[2 + k][:, (t - 2) * 256:(t - 1) * 256], lhs[:, s, t * P:(t + 1) * P],
                                                rhs[:, s, :], start=True, stop=True)
                    last.then_inc(pre_b, 1)
                    pe.wait_ge(rows_in[s], (i + 1) * (16 * TPG))
                    if late(g, 2):
                        pe.wait_ge(fin, g - 1)
                    for t in (0, 1):
                        place = bank[k][:, t * 256:(t + 1) * 256]
                        nc.tensor.matmul(place, lhs[:, s, t * P:(t + 1) * P], rhs[:, s, :], start=True, stop=False)
                        last = nc.tensor.matmul(place, ident[:, :], got[:, s, t, :], start=False, stop=True)
                    last.then_inc(pre_a, 1)

                def sums(g, s, i, _):
                    k = s % 2
                    pe.wait_ge(fin, g + 1)
                    if late(g, 2):
                        pe.wait_ge(accd, g - 1)
                    for t in range(TPG):
                        nc.tensor.matmul(bank[4 + k][:, 0:W], msg[:, k, t, :], hot[:, k, t, :],
                                         start=(t == 0), stop=(t == TPG - 1))
                    hot_bf = hot[:, k, :, :].bitcast(bf16).rearrange("p t (w h) -> p t w h", h=2)
                    for t in range(TPG):
                        last = nc.tensor.matmul(bank[4 + k][:, W:2 * W], ones_bf[:, :], hot_bf[:, t, :, 1],
                                                start=(t == 0), stop=(t == TPG - 1))
                    last.then_inc(summed, 1)
                groups(pe, [(products, 0), (sums, 2)])

            def fast1():
                def sums(g, s, i, _):
                    k = s % 2
                    pe.wait_ge(rows1_in[s], (i + 1) * (16 * TPG))
                    pe.wait_ge(hot1_ready, g + 1)
                    if late(g, 2):
                        pe.wait_ge(accd1, g - 1)
                    for t in range(TPG):
                        last = nc.tensor.matmul(bank[4 + k][:, 0:W], got[:, s, t, 0:C], hot[:, k, t, :],
                                                start=(t == 0), stop=(t == TPG - 1))
                    last.then_inc(summed1, 1)
                groups(pe, [(sums, 0)])

            verdict = sorted_enough(pe)
            with pe.If(verdict == P):
                fast0()
            with pe.Else():
                general_pe(pe, 0)

            pe.wait_ge(edges_done[0], 1)
            def count_block(b, j):
                pe.wait_ge(n_slot, b + 1)
                nc.tensor.matmul(bank[6][:, bass.ds(b, 1)], slot_b[:, j, :], avg[:, :], start=True, stop=True).then_inc(n_prod, 1)
            blocks2(pe, count_block)
            def sum_block(b, j):
                pe.wait_ge(n_slot2, b + 1)
                if late(b, 2):
                    pe.wait_ge(n_used2, b - 1)
                nc.tensor.transpose(bank[j][:, 0:C], slot_a[:, j, :], ident[:, :]).then_inc(n_prod2, 1)
            blocks2(pe, sum_block)
            for n, step in enumerate((STEP_SUM, STEP_SQ)):
                pe.wait_ge(dve_step, step)
                nc.tensor.matmul(bank[7][:, 0:C], inv_n[:, :], chan[:, 0, :], start=True, stop=True).then_inc(pe_step, 1)

            with pe.If(verdict == P):
                fast1()
            with pe.Else():
                general_pe(pe, 1)
            pe.wait_ge(edges_done[1], 1)
            def final_block(b, j):
                pe.wait_ge(f_slot, b + 1)
                if late(b, 2):
                    pe.wait_ge(f_bias, b - 1)
                nc.tensor.matmul(bank[j][:, 0:C], slot_a[:, j, :], w1_s[:, :], start=True, stop=True).then_inc(f_prod, 1)
            blocks2(pe, final_block)


_OUT = ("out_dram", (NP, C), "float32")


def kernel(**inputs):
    import numpy as np
    import concourse.bacc as bacc
    from concourse.bass_utils import run_bass_kernel_spmd

    a = {k: np.asarray(v) for k, v in inputs.items()}
    x = np.zeros((NP, C), a["x"].dtype)
    x[:N] = a["x"]
    src = np.zeros(G * GE, a["src"].dtype)
    src[:E] = a["src"]
    dst = np.full(G * GE, N, a["dst"].dtype)
    dst[:E] = a["dst"]
    edge = np.zeros((G * GE, D), a["edge_attr_64"].dtype)
    edge[:E] = a["edge_attr_64"]
    arrays = {
        "x": x,
        "src": src.reshape(G, TPG, P).transpose(0, 2, 1),
        "dst_cols": dst.reshape(TILES, P).T,
        "dst_row": dst.reshape(G, GE),
        "dst_first": dst[::GE],
        "edge_t": edge.reshape(G, GE, D).transpose(0, 2, 1),
        "wf_t": a["L0_gnn_W_f"].T,
        "ws_t": a["L0_gnn_W_s"].T,
        "bf": a["L0_gnn_b_f"],
        "bs": a["L0_gnn_b_s"],
        "gamma": a["L0_gnn_gamma"],
        "beta": a["L0_gnn_beta"],
        "w1": a["L1_gnn_W"],
        "b1": a["L1_gnn_b"],
    }
    arrays = {f"in_{k}": np.ascontiguousarray(v) for k, v in arrays.items()}
    nc = bacc.Bacc("TRN2", target_bir_lowering=False, num_devices=1)
    args = [nc.dram_tensor(k, v.shape, mybir.dt.from_np(v.dtype), kind="ExternalInput").ap() for k, v in arrays.items()]
    name, shape, dtype = _OUT
    out = nc.dram_tensor(name, shape, mybir.dt.from_np(np.dtype(dtype)), kind="ExternalOutput").ap()
    program(nc, *args, out)
    r = run_bass_kernel_spmd(nc, [arrays], core_ids=[0])
    return r.results[0][name][:N]
```

```python
import concourse.bass as bass
from concourse import mybir
from contextlib import ExitStack

N = 6250
C = 128
D = 64
E = 206250
P = 128
NB = 50
NP = NB * P
TPG = 4
GE = TPG * P
SLOTS = 4
G = -(-E // (GE * SLOTS)) * SLOTS
ITERS = G // SLOTS
TILES = G * TPG
W = 64
GATHERED = SLOTS
COUNTED = 5
UNIT = GATHERED + COUNTED
UNITS = -(-G // UNIT)
CT = COUNTED * TPG
TW = 8
HB = -(-N // P)
KEYS = HB * TW
PARTS = 3
GA = UNITS * UNIT
TA = GA * TPG
AW = C + 1
EPS = 1e-5
EXP_LN = "natural_log_exp_and_others"
STEP_CEN, STEP_VAR, STEP_H = 3, 5, 21
STEP_DEG, STEP_SUM, STEP_BN_CEN, STEP_SQ, STEP_BN_VAR = 23, 29, 34, 35, 36
STEP_CEN2, STEP_VAR2, STEP_T = 43, 45, 48
STEP_ACT_SQ2 = 6


def program(nc, x, src, dst_cols, dst_row, dst_first, dst_first_t, src_cols, edge_t, wf_t, ws_t, bf, bs, gamma, beta, w1, b1, out):
    f32, i32, bf16, f16 = mybir.dt.float32, mybir.dt.int32, mybir.dt.bfloat16, mybir.dt.float16
    ALU, ACT, AX = mybir.AluOpType, mybir.ActivationFunctionType, mybir.AxisListType

    table_dst = nc.dram_tensor("table_dst", (NP, 2 * C), f32).ap()
    table_src = nc.dram_tensor("table_src", (NP, 2 * C), f32).ap()
    table_gcn = nc.dram_tensor("table_gcn", (NP, C), f32).ap()
    x1_rows = nc.dram_tensor("x1_rows", (NP, C), f32).ap()
    acc_rows = [nc.dram_tensor(f"acc_rows{i}", (NP, AW), f32).ap() for i in range(2)]

    x_v = x.rearrange("(b p) c -> p b c", p=P)
    gcn_v = table_gcn.rearrange("(b p) c -> p b c", p=P)

    ctx = ExitStack()
    with ctx:
        def sb(name, shape, dt=f32):
            return ctx.enter_context(nc.sbuf_tensor(name, shape, dt))

        def sem(name):
            return ctx.enter_context(nc.semaphore(name))

        def sems(name, n):
            return [sem(f"{name}{i}") for i in range(n)]

        x_rows = sb("x_rows", [P, NB, C])
        h_rows = sb("h_rows", [P, NB, C])
        acc = sb("acc", [P, 2, NP])
        scratch = acc[:, 0, :].rearrange("p (b c) -> p b c", c=C)
        dst_rel = sb("dst_rel", [P, TA])
        first_i = sb("first_i", [P, GA], i32)
        first_f = sb("first_f", [P, GA])
        first_t = sb("first_t", [P, TA], i32)
        key = sb("key", [P, TA], f16)
        low = sb("low", [P, TA], f16)
        iota_k = sb("iota_k", [P, KEYS], f16)
        hot_k = sb("hot_k", [P, 4, KEYS], f16)
        hot_l = sb("hot_l", [P, 4, P], f16)
        ident = sb("ident", [P, P])
        iota_w = sb("iota_w", [P, W])
        iota_p = sb("iota_p", [P, 1])
        row_id = sb("row_id", [P, 1])
        ones_bf = sb("ones_bf", [P, P], bf16)
        inv_n = sb("inv_n", [P, P])
        avg = sb("avg", [P, 1])
        ones = sb("ones", [P, 1])
        below = sb("below", [P, P])
        w_nodes = sb("w_nodes", [P, 4 * C])
        w_edge = sb("w_edge", [D, 2 * C])
        bias = sb("bias", [P, 2 * C])
        gamma_b = sb("gamma_b", [P, C])
        beta_b = sb("beta_b", [P, C])
        w1_s = sb("w1_s", [P, C])
        b1_b = sb("b1_b", [P, C])
        stat = sb("stat", [P, 8, NB])
        chan = sb("chan", [P, 4, C])
        flag_c = sb("flag_c", [P, 4])
        flags = sb("flags", [P, 8])
        flag_i = sb("flag_i", [1, 1], i32)
        slot_a = sb("slot_a", [P, 2, C])
        slot_b = sb("slot_b", [P, 2, C])
        slot_o = sb("slot_o", [P, 2, 4 * C])
        src_i = sb("src_i", [P, SLOTS, TPG], i32)
        got = sb("got", [P, SLOTS, TPG, 2 * C])
        hot = sb("hot", [P, 2, TPG, W])
        parts_words = PARTS * HB * C // 2
        ring = sb("ring", [P, max(parts_words, 2 * SLOTS * GE + SLOTS * 2 * C + 16 * C + 2 * TPG * C)])
        at = [0]

        def carve(words, dims, **sizes):
            at[0] += words
            return ring[:, at[0] - words:at[0]].rearrange(f"p ({dims}) -> p {dims}", **sizes)
        lhs = carve(SLOTS * GE, "s e", s=SLOTS)
        rhs_w = sb("rhs", [P, SLOTS, 2 * C])
        rhs = rhs_w[:, :, :]
        dst_b = carve(SLOTS * GE, "s e", s=SLOTS).bitcast(i32)
        pre = carve(8 * C, "k t c", k=2, t=2)
        uv = carve(4 * TPG * C, "k t c", k=2, t=TPG)
        msg = carve(2 * TPG * C, "k t c", k=2, t=TPG)
        dst_i, src_a, rel_t = (ring[:, n * TA:(n + 1) * TA] for n in range(3))
        dst_i, src_a = dst_i.bitcast(i32), src_a.bitcast(i32)
        whole = ring[:, 3 * TA:4 * TA].bitcast(i32)
        gcn_parts = ring[:, 0:parts_words].bitcast(bf16).rearrange("p (q b c) -> p q b c", q=PARTS, b=HB)
        adj = [words[:, 0:HB * CT * TW // 2].bitcast(f16).rearrange("p (b t w) -> p b t w", b=HB, t=CT)
               for words in (acc[:, 1, :], x_rows[:, :, :].rearrange("p b c -> p (b c)"))]
        bank = [ctx.enter_context(nc.psum_tensor(f"bank{i}", [P, 512], f32)) for i in range(8)]

        x_in, consts_in, index_in, pool_consts = sem("x_in"), sem("consts_in"), sem("index_in"), sem("pool_consts")
        weights_ready, flag_ok, flag_sum, flag_ready = sem("weights_ready"), sem("flag_ok"), sem("flag_sum"), sem("flag_ready")
        dve_step, act_step, pe_step = sem("dve_step"), sem("act_step"), sem("pe_step")
        acc_zero, acc_zero1 = sem("acc_zero"), sem("acc_zero1")
        t_copied, t_turned, t_slot, t_made, t_dst, t_src = (sem(n) for n in (
            "t_copied", "t_turned", "t_slot", "t_made", "t_dst", "t_src"))
        t_stored = sems("t_stored", 2)
        edge_in, srcs_in, rows_in = sems("edge_in", SLOTS), sems("srcs_in", SLOTS), sems("rows_in", SLOTS)
        onehot_t, pre_b, pre_a, added, act_done, fin, val_a, hot_ready, summed, accd = (sem(n) for n in (
            "onehot_t", "pre_b", "pre_a", "added", "act_done", "fin", "val_ready", "hot_ready", "summed", "accumulated"))
        act_chain = sem("act_chain")
        edges_done = sems("edges_done", 2)
        n_slot, n_prod, n_used, n_slot2, n_prod2, n_used2 = (sem(n) for n in (
            "n_slot", "n_prod", "n_used", "n_slot2", "n_prod2", "n_used2"))
        gcn_stored = sem("gcn_stored")
        srcs1_in, rows1_in = sems("srcs1_in", SLOTS), sems("rows1_in", SLOTS)
        hot1_ready, summed1, accd1 = sem("hot1_ready"), sem("summed1"), sem("accumulated1")
        keys_ready, x1_stored, part_ready, rest_ready = sem("keys_ready"), sem("x1_stored"), sem("part_ready"), sem("rest_ready")
        c_hot, c_counted, c_evac, c_product, c_added = (sem(n) for n in (
            "c_hot", "c_counted", "c_evac", "c_product", "c_added"))
        x1_in = sems("x1_in", 2)
        f_slot, f_prod, f_bias, f_out = sem("f_slot"), sem("f_prod"), sem("f_bias"), sem("f_out")
        out_stored = sems("out_stored", 2)
        beta_added, waits_taken = sem("beta_added"), sem("waits_taken")
        g_in, g_rows, g_pre, g_half, g_add, g_actc, g_act, g_msg, g_sum, g_index, g_out, g_scat, g_dve, g_one = (
            sems(n, 2) for n in ("g_in", "g_rows", "g_pre", "g_half", "g_add", "g_actc", "g_act", "g_msg", "g_sum",
                                 "g_index", "g_out", "g_scat", "g_dve", "g_one"))
        g_back, g_turned, g_turn, g_zeroed = (sems(n, 2) for n in ("g_back", "g_turned", "g_turn", "g_zeroed"))

        block = ctx.enter_context(nc.Block())

        def blocks2(eng, step):
            for j in range(2):
                step(j, j)
            with eng.Fori(1, NB // 2) as i:
                for j in range(2):
                    step(i * 2 + j, j)

        def groups(eng, stages, before=None, iters=ITERS):
            def body(i):
                regs = before(i) if before else None
                for s in range(SLOTS):
                    for stage, lag in stages:
                        turn, at = (i, s - lag) if s >= lag else (i - 1, s - lag + SLOTS)
                        if isinstance(turn, int) and turn < 0:
                            continue
                        stage(turn * SLOTS + at, at, turn, regs and regs[s])
            body(0)
            with eng.Fori(1, iters) as i:
                body(i)
            most = max(lag for _, lag in stages)
            regs = before(iters) if before and most else None
            for d in range(most):
                for stage, lag in stages:
                    if d < lag:
                        g = iters * SLOTS + d - lag
                        stage(g, g % SLOTS, iters - 1, regs and regs[d])

        def firsts(engine, lag):
            def load(i):
                at = i * SLOTS - lag
                skip = max(0, -at) if isinstance(i, int) else 0
                n = min(SLOTS, G - at) if isinstance(i, int) else SLOTS
                _, regs = nc.values_load_multi_w_load_instructions(
                    first_i[0:1, bass.ds(at + skip, n - skip)], engines=(engine,), min_val=0, max_val=N,
                    skip_runtime_bounds_check_because="a dst is a node, or N for the padding")
                return [None] * skip + list(regs)
            return load

        def units(eng, body):
            assert UNITS % 2 == 1
            body(1, 1)
            body(2, 0)
            with eng.Fori(1, UNITS // 2) as i:
                body(i * 2 + 1, 1)
                body(i * 2 + 2, 0)

        def late(g, n):
            return not isinstance(g, int) or g >= n

        def take_waits(eng):
            eng.sem_inc(waits_taken, 1)

        def sorted_enough(eng):
            eng.wait_ge(flag_ready, 1)
            return eng.value_load(flag_i[0:1, 0:1], min_val=0, max_val=P)

        def tiles(eng, step):
            for j in range(TPG):
                step(0, j, j)
            with eng.Fori(1, G) as g:
                for j in range(TPG):
                    step(g, j, g * TPG + j)

        g_same = hot[:, 0, :, :].rearrange("p t w -> p (t w)")[:, 0:P]
        g_before = hot[:, 1, :, :].rearrange("p t w -> p (t w)")[:, 0:P]
        g_msg_rows = uv[:, 1, 0, 0:AW]
        g_sum_rows = uv[:, 1, 1, 0:AW]
        g_uv = uv[:, 0, 0, :]
        g_col = flag_c
        g_dst, g_src, g_to = src_i[:, 1, 0:1], src_i[:, 0, 0:1], src_i[:, 2, 0:1]
        loads = (4, 3)

        def general_sync(sp, layer):
            sp.wait_ge(keys_ready, 1)
            sp.wait_ge((acc_zero, acc_zero1)[layer], 1)
            sp.dma_start(acc_rows[layer].rearrange("(b p) a -> p b a", p=P),
                         acc[:, 0, 0:AW].unsqueeze(1).to_broadcast([P, NB, AW])).then_inc(g_zeroed[layer], 16)
            sp.wait_ge(g_zeroed[layer], 16)

            def load(g, j, t):
                at = sp.snap(t) if not isinstance(t, int) else t
                if late(t, 1):
                    sp.wait_ge(g_scat[layer], t * 16)
                    take_waits(sp)
                sp.dma_start(g_src, src[bass.ds(g, 1), :, j:j + 1].rearrange("a p t -> (a p) t"),
                             allow_slow_non_contiguous=True).then_inc(g_in[layer], 16)
                sp.dma_start(g_dst, dst_cols[:, bass.ds(at, 1)], allow_slow_non_contiguous=True).then_inc(g_in[layer], 16)
                sp.dma_start(dst_b[:, 0, 0:P], dst_row[bass.ds(g, 1), j * P:(j + 1) * P].rearrange("a e -> (a e)")
                             .partition_broadcast(P)).then_inc(g_in[layer], 16)
                if layer == 0:
                    sp.dma_start(lhs[0:D, 0, 0:P], edge_t[bass.ds(g, 1), :, j * P:(j + 1) * P]
                                 .rearrange("a k e -> (a k) e")).then_inc(g_in[layer], 16)
            tiles(sp, load)
            sp.wait_ge(g_scat[layer], 16 * TILES)
            def back(b, j):
                rows = sp.snap(b * P) if not isinstance(b, int) else b * P
                if late(b, 1):
                    sp.wait_ge(g_turn[layer], b)
                take_waits(sp)
                sp.dma_start(slot_o[:, j, 0:AW], acc_rows[layer][bass.ds(rows, P), :]).then_inc(g_back[layer], 16)
            blocks2(sp, back)

        def general_pool(pool, layer):
            def move(g, j, t):
                pool.wait_ge(g_in[layer], (t + 1) * (16 * loads[layer]))
                take_waits(pool)
                if layer == 0:
                    pool.indirect_dma_start(out=got[:, 0, 0, :], out_offset=None, in_=table_dst,
                                            in_offset=bass.IndirectOffsetOnAxis(ap=g_dst, axis=0)).then_inc(g_rows[layer], 16)
                table, width = ((table_src, 2 * C), (table_gcn, C))[layer]
                pool.indirect_dma_start(out=got[:, 0, 1, 0:width], out_offset=None, in_=table,
                                        in_offset=bass.IndirectOffsetOnAxis(ap=g_src, axis=0)).then_inc(g_rows[layer], 16)
                pool.wait_ge(g_out[layer], t + 1)
                take_waits(pool)
                pool.indirect_dma_start(out=acc_rows[layer], out_offset=bass.IndirectOffsetOnAxis(ap=g_to, axis=0),
                                        in_=g_sum_rows, in_offset=None, compute_op=ALU.add).then_inc(g_scat[layer], 16)
            tiles(pool, move)

        def general_act(act, layer):
            if layer:
                return
            u, v = g_uv[:, 0:C], g_uv[:, C:2 * C]
            nc.scalar.preload_act_table_set(EXP_LN)
            def acts(g, j, t):
                act.wait_ge(g_add[0], t + 1)
                nc.scalar.activation(u, pre[:, 0, 1, 0:C], ACT.Exp).then_inc(g_actc[0], 1)
                nc.scalar.activation(v, pre[:, 0, 1, C:2 * C], ACT.Abs).then_inc(g_actc[0], 1)
                act.wait_ge(g_actc[0], t * 4 + 2)
                nc.scalar.activation(v, v, ACT.Exp, scale=-1.0).then_inc(g_actc[0], 1)
                act.wait_ge(g_actc[0], t * 4 + 3)
                nc.scalar.activation(g_uv, g_uv, ACT.Ln, bias=1.0).then_inc(g_actc[0], 1)
                act.wait_ge(g_actc[0], t * 4 + 4)
                nc.scalar.activation(u, u, ACT.Exp, scale=-1.0).then_inc(g_act[0], 1)
            tiles(act, acts)

        def general_dve(dve, layer):
            n_links = (7, 6)[layer]
            link_sem = g_dve[layer]
            nc.vector.memset(g_msg_rows[:, C:AW], 1.0).then_inc(g_one[layer], 1)
            nc.vector.tensor_scalar(g_col[:, 3:4], row_id[:, :], float(N + 1), None, ALU.add).then_inc(g_one[layer], 1)
            dve.wait_ge(g_one[layer], 2)

            def work(g, j, t):
                made = [0]

                def link(ins):
                    made[0] += 1
                    ins.then_inc(link_sem, 1)
                    dve.wait_ge(link_sem, t * n_links + made[0])

                dve.wait_ge(g_in[layer], (t + 1) * (16 * loads[layer]))
                link(nc.vector.tensor_copy(g_col[:, 0:1], g_dst))
                link(nc.vector.tensor_scalar(g_same, dst_b[:, 0, 0:P], g_col[:, 0:1], None, ALU.is_equal))
                link(nc.vector.tensor_tensor(g_before, g_same, below[:, :], ALU.mult))
                link(nc.vector.tensor_reduce(g_col[:, 1:2], g_before, AX.X, ALU.add))
                link(nc.vector.tensor_scalar(g_col[:, 2:3], g_col[:, 1:2], 0.0, None, ALU.is_equal))
                link(nc.vector.tensor_scalar(g_col[:, 1:2], g_col[:, 0:1], g_col[:, 3:4], g_col[:, 2:3],
                                             ALU.subtract, ALU.mult))
                nc.vector.tensor_tensor(g_to, g_col[:, 1:2], g_col[:, 3:4], ALU.add).then_inc(g_index[layer], 1)
                dve.wait_ge(g_rows[layer], (t + 1) * (32, 16)[layer])
                if layer == 0:
                    dve.wait_ge(g_pre[0], t + 1)
                    nc.vector.tensor_tensor(pre[:, 0, 0, :], bank[2][:, 0:2 * C], got[:, 0, 0, :], ALU.add
                                            ).then_inc(g_half[0], 1)
                    dve.wait_ge(g_half[0], t + 1)
                    nc.vector.tensor_tensor(pre[:, 0, 1, :], pre[:, 0, 0, :], got[:, 0, 1, :], ALU.add
                                            ).then_inc(g_add[0], 1)
                    dve.wait_ge(g_act[0], t + 1)
                    link(nc.vector.scalar_tensor_tensor(out=g_uv[:, C:2 * C], in0=pre[:, 0, 1, C:2 * C], scalar=0.0,
                                                        in1=g_uv[:, C:2 * C], op0=ALU.max, op1=ALU.add))
                    nc.vector.tensor_tensor(g_msg_rows[:, 0:C], g_uv[:, C:2 * C], g_uv[:, 0:C], ALU.mult
                                            ).then_inc(g_msg[0], 1)
                else:
                    nc.vector.tensor_copy(g_msg_rows[:, 0:C], got[:, 0, 1, 0:C]).then_inc(g_msg[1], 1)
                assert made[0] == n_links
                dve.wait_ge(g_sum[layer], t + 1)
                dve.wait_ge(g_index[layer], t + 1)
                nc.vector.tensor_copy(g_sum_rows, bank[4][:, 0:AW]).then_inc(g_out[layer], 1)
            tiles(dve, work)
            def back(b, j):
                dve.wait_ge(g_turned[layer], b + 1)
                nc.vector.tensor_copy(acc[:, :, bass.ds(b * P, P)], bank[j][:, 0:2 * P].rearrange("p (a n) -> p a n", a=2)
                                      ).then_inc(g_turn[layer], 1)
            blocks2(dve, back)
            dve.wait_ge(g_turn[layer], NB)

        def general_pe(pe, layer):
            def work(g, j, t):
                if layer == 0:
                    pe.wait_ge(g_in[0], (t + 1) * (16 * loads[0]))
                    nc.tensor.matmul(bank[2][:, 0:2 * C], lhs[0:D, 0, 0:P], rhs[0:D, 0, :], start=True, stop=True
                                     ).then_inc(g_pre[0], 1)
                pe.wait_ge(g_msg[layer], t + 1)
                nc.tensor.matmul(bank[4][:, 0:AW], g_same, g_msg_rows, start=True, stop=True).then_inc(g_sum[layer], 1)
            tiles(pe, work)
            def back(b, j):
                pe.wait_ge(g_back[layer], (b + 1) * 16)
                if late(b, 2):
                    pe.wait_ge(g_turn[layer], b - 1)
                nc.tensor.transpose(bank[j][:, 0:P], slot_o[:, j, 0:C], ident[:, :])
                nc.tensor.matmul(bank[j][:, P:2 * P], slot_o[:, j, C:AW].to_broadcast([P, P]), ident[:, :],
                                 start=True, stop=True).then_inc(g_turned[layer], 1)
            blocks2(pe, back)

        @block.sync
        def _(sp):
            sp.dma_start(x_rows[:, :, :], x_v).then_inc(x_in, 16)
            sp.dma_start(dst_i, dst_cols).then_inc(index_in, 16)
            sp.dma_start(src_a, src_cols).then_inc(index_in, 16)
            sp.dma_start(first_i[:, :], dst_first.partition_broadcast(P)).then_inc(index_in, 16)
            sp.dma_start(first_t[:, :], dst_first_t.partition_broadcast(P)).then_inc(index_in, 16)
            for k, part in enumerate((wf_t[0:C], ws_t[0:C], wf_t[C:2 * C], ws_t[C:2 * C])):
                sp.dma_start(w_nodes[:, k * C:(k + 1) * C], part).then_inc(consts_in, 16)
            sp.dma_start(w_edge[:, 0:C], wf_t[2 * C:2 * C + D]).then_inc(consts_in, 16)
            sp.dma_start(w_edge[:, C:2 * C], ws_t[2 * C:2 * C + D]).then_inc(consts_in, 16)
            for tile, row in ((bias[:, 0:C], bf), (bias[:, C:2 * C], bs), (gamma_b[:, :], gamma),
                              (beta_b[:, :], beta), (b1_b[:, :], b1)):
                sp.dma_start(tile, row.partition_broadcast(P)).then_inc(consts_in, 16)
            sp.dma_start(w1_s[:, :], w1).then_inc(consts_in, 16)

            def store_tables(b, j):
                rows = sp.snap(b * P) if not isinstance(b, int) else b * P
                n = b + 1
                sp.wait_ge(t_dst, n)
                sp.wait_ge(t_src, n)
                sp.dma_start(table_dst[bass.ds(rows, P), :], slot_o[:, j, 0:2 * C]).then_inc(t_stored[j], 16)
                sp.dma_start(table_src[bass.ds(rows, P), :], slot_o[:, j, 2 * C:4 * C]).then_inc(t_stored[j], 16)
            blocks2(sp, store_tables)
            for j in range(2):
                sp.wait_ge(t_stored[j], 16 * NB)

            def fast0():
                sp.wait_ge(keys_ready, 1)
                def load_edges(g, s, i, first):
                    if late(g, SLOTS):
                        sp.wait_ge(pre_a, g - SLOTS + 1)
                    sp.dma_start(lhs[0:D, s, :], edge_t[bass.ds(g, 1)].rearrange("a k e -> (a k) e")).then_inc(edge_in[s], 16)
                    sp.dma_start(dst_b[D:P, s, :], dst_row[bass.ds(g, 1), :].rearrange("a e -> (a e)")
                                 .partition_broadcast(W)).then_inc(edge_in[s], 16)
                    sp.dma_start(rhs[D:P, s, :], table_dst[bass.ds(first, W), :]).then_inc(edge_in[s], 16)
                    if late(g, SLOTS):
                        sp.wait_ge(rows_in[s], i * (16 * TPG))
                    sp.dma_start(src_i[:, s, :], src[bass.ds(g, 1)].rearrange("a p t -> (a p) t")).then_inc(srcs_in[s], 16)
                groups(sp, [(load_edges, 0)], firsts(mybir.EngineType.SP, 0))

            def fast1():
                def load_srcs(g, s, i, _):
                    if late(g, SLOTS):
                        sp.wait_ge(rows1_in[s], i * (16 * TPG))
                    at = i * UNIT + s
                    sp.dma_start(src_i[:, s, :], src[bass.ds(at, 1)].rearrange("a p t -> (a p) t")).then_inc(srcs1_in[s], 16)
                groups(sp, [(load_srcs, 0)], iters=UNITS)

            verdict = sorted_enough(sp)
            with sp.If(verdict == P):
                fast0()
            with sp.Else():
                general_sync(sp, 0)
            sp.wait_ge(dve_step, STEP_T)
            sp.dma_start(gcn_v, h_rows[:, :, :]).then_inc(gcn_stored, 16)
            sp.dma_start(x1_rows.rearrange("(b p) c -> p b c", p=P), x_rows[:, :, :]).then_inc(x1_stored, 16)
            sp.wait_ge(gcn_stored, 16)
            with sp.If(verdict == P):
                fast1()
            with sp.Else():
                general_sync(sp, 1)

            sp.wait_ge(x1_stored, 16)
            def store_out(b, j):
                rows = sp.snap(b * P) if not isinstance(b, int) else b * P
                if late(b, 2):
                    sp.wait_ge(f_out, b - 1)
                    take_waits(sp)
                sp.dma_start(slot_o[:, j, 2 * C:3 * C], x1_rows[bass.ds(rows, P), :]).then_inc(x1_in[j], 16)
                sp.wait_ge(f_out, b + 1)
                sp.dma_start(out[bass.ds(rows, P), :], slot_o[:, j, C:2 * C]).then_inc(out_stored[j], 16)
            blocks2(sp, store_out)
            for j in range(2):
                sp.wait_ge(out_stored[j], 16 * (NB // 2))

        @block.gpsimd
        def _(pool):
            nc.gpsimd.memset(ident[:, :], 0.0).then_inc(pool_consts, 1)
            nc.gpsimd.memset(below[:, :], 1.0).then_inc(pool_consts, 1)
            nc.gpsimd.memset(ones_bf[:, :], 1.0).then_inc(pool_consts, 1)
            nc.gpsimd.memset(inv_n[:, :], 1.0 / N).then_inc(pool_consts, 1)
            nc.gpsimd.memset(avg[:, :], 1.0 / P).then_inc(pool_consts, 1)
            nc.gpsimd.memset(ones[:, :], 1.0).then_inc(pool_consts, 1)
            nc.gpsimd.iota(iota_w[:, :], pattern=[[1, W]], base=0, channel_multiplier=0,
                           allow_small_or_imprecise_dtypes=True).then_inc(pool_consts, 1)
            nc.gpsimd.iota(iota_p[:, :], pattern=[[0, 1]], base=-(P - W), channel_multiplier=1,
                           allow_small_or_imprecise_dtypes=True).then_inc(pool_consts, 1)
            nc.gpsimd.iota(row_id[:, :], pattern=[[0, 1]], base=0, channel_multiplier=1,
                           allow_small_or_imprecise_dtypes=True).then_inc(pool_consts, 1)
            nc.gpsimd.iota(iota_k[:, :], pattern=[[1, KEYS]], base=0, channel_multiplier=0,
                           allow_small_or_imprecise_dtypes=True).then_inc(pool_consts, 1)
            pool.wait_ge(pool_consts, 10)
            nc.gpsimd.affine_select(out=ident[:, :], in_=ident[:, :], compare_op=ALU.not_equal, fill=1.0, base=0,
                                    pattern=[[-1, P]], channel_multiplier=1).then_inc(pool_consts, 1)
            nc.gpsimd.affine_select(out=below[:, :], in_=below[:, :], compare_op=ALU.is_gt, fill=0.0, base=0,
                                    pattern=[[-1, P]], channel_multiplier=1).then_inc(pool_consts, 1)

            pool.wait_ge(dve_step, STEP_H)
            def copy_h(b, j):
                if late(b, 2):
                    pool.wait_ge(t_turned, b - 1)
                nc.gpsimd.tensor_copy(slot_a[:, j, :], h_rows[:, bass.ds(b, 1), :].rearrange("p a c -> p (a c)")
                                      ).then_inc(t_copied, 1)
            blocks2(pool, copy_h)
            pool.wait_ge(act_step, 1)
            pool.wait_ge(dve_step, STEP_VAR)
            nc.gpsimd.memset(acc[:, :, :], 0.0).then_inc(acc_zero, 1)
            for j in range(2):
                pool.wait_ge(t_stored[j], 16 * NB)

            def gathers(table, width, rows, srcs, used, iters):
                def gather(g, s, i, _):
                    pool.wait_ge(srcs[s], (i + 1) * 16)
                    if late(g, SLOTS):
                        for done in used:
                            pool.wait_ge(done, g - SLOTS + 1)
                    take_waits(pool)
                    for t in range(TPG):
                        pool.indirect_dma_start(
                            out=got[:, s, t, 0:width], out_offset=None, in_=table,
                            in_offset=bass.IndirectOffsetOnAxis(ap=src_i[:, s, t:t + 1], axis=0)).then_inc(rows[s], 16)
                groups(pool, [(gather, 0)], iters=iters)

            verdict = sorted_enough(pool)
            with pool.If(verdict == P):
                gathers(table_src, 2 * C, rows_in, srcs_in, (pre_a, added), ITERS)
            with pool.Else():
                general_pool(pool, 0)
            pool.wait_ge(edges_done[0], 1)
            pool.wait_ge(consts_in, 16 * 12)
            nc.gpsimd.tensor_tensor(x_rows[:, :, :], x_rows[:, :, :],
                                    beta_b[:, :].unsqueeze(1).to_broadcast([P, NB, C]), ALU.add).then_inc(beta_added, 1)
            pool.wait_ge(act_step, STEP_ACT_SQ2)
            pool.wait_ge(dve_step, STEP_T)
            nc.gpsimd.memset(acc[:, 0, :], 0.0).then_inc(acc_zero1, 1)
            pool.wait_ge(gcn_stored, 16)
            with pool.If(verdict == P):
                gathers(table_gcn, C, rows1_in, srcs1_in, (summed1,), UNITS)
            with pool.Else():
                general_pool(pool, 1)

        @block.scalar
        def _(act):
            act.wait_ge(consts_in, 16 * 12)
            for part in (w_nodes[:, 0:C], w_nodes[:, 2 * C:3 * C], bias[:, 0:C]):
                nc.scalar.mul(part, part, -1.0).then_inc(weights_ready, 1)
            for s in range(SLOTS):
                nc.scalar.mul(rhs[0:D, s, 0:C], w_edge[:, 0:C], -1.0).then_inc(weights_ready, 1)
                nc.scalar.copy(rhs[0:D, s, C:2 * C], w_edge[:, C:2 * C]).then_inc(weights_ready, 1)

            def square(step, count):
                act.wait_ge(dve_step, step)
                nc.scalar.activation(scratch, h_rows[:, :, :], ACT.Square).then_inc(act_step, 1)

            def root(step, ap):
                act.wait_ge(dve_step, step)
                nc.scalar.activation(ap, ap, ACT.Sqrt).then_inc(act_step, 1)

            square(STEP_CEN, 1)
            root(STEP_VAR, stat[:, 2, :])

            def tables(b, j):
                act.wait_ge(t_turned, b + 1)
                if late(b, 2):
                    act.wait_ge(t_made, b - 1)
                nc.scalar.copy(slot_b[:, j, :], bank[j][:, 0:C]).then_inc(t_slot, 1)
                act.wait_ge(t_made, b + 1)
                if late(b, 2):
                    act.wait_ge(t_stored[j], (b - j) * 16)
                nc.scalar.copy(slot_o[:, j, 2 * C:4 * C], bank[4 + j][:, 0:2 * C]).then_inc(t_src, 1)
            blocks2(act, tables)

            def fast0():
                nc.scalar.preload_act_table_set(EXP_LN)
                def acts(g, s, i, _):
                    k = s % 2
                    u, v = uv[:, k, :, 0:C], uv[:, k, :, C:2 * C]
                    act.wait_ge(added, g + 1)
                    if late(g, 2):
                        act.wait_ge(fin, g - 1)
                    nc.scalar.activation(u[:, 2:4, :], pre[:, k, :, 0:C], ACT.Exp).then_inc(act_chain, 1)
                    nc.scalar.activation(v[:, 2:4, :], pre[:, k, :, C:2 * C], ACT.Abs).then_inc(act_chain, 1)
                    act.wait_ge(pre_a, g + 1)
                    pa = bank[k][:, :].rearrange("p (t c) -> p t c", t=2)
                    nc.scalar.activation(u[:, 0:2, :], pa[:, :, 0:C], ACT.Exp).then_inc(act_chain, 1)
                    nc.scalar.activation(v[:, 0:2, :], pa[:, :, C:2 * C], ACT.Abs).then_inc(act_chain, 1)
                    act.wait_ge(act_chain, g * 6 + 4)
                    nc.scalar.activation(v, v, ACT.Exp, scale=-1.0).then_inc(act_chain, 1)
                    act.wait_ge(act_chain, g * 6 + 5)
                    nc.scalar.activation(uv[:, k, :, :], uv[:, k, :, :], ACT.Ln, bias=1.0).then_inc(act_chain, 1)
                    act.wait_ge(act_chain, g * 6 + 6)
                    nc.scalar.activation(u, u, ACT.Exp, scale=-1.0).then_inc(act_done, 1)
                groups(act, [(acts, 0)])

            verdict = sorted_enough(act)
            with act.If(verdict == P):
                fast0()
            with act.Else():
                general_act(act, 0)

            act.wait_ge(edges_done[0], 1)
            def count_block(b, j):
                if late(b, 2):
                    act.wait_ge(n_prod, b - 1)
                nc.scalar.copy(slot_b[:, j, :], acc[:, 1, bass.ds(b * P, P)]).then_inc(n_slot, 1)
            blocks2(act, count_block)
            def sum_block(b, j):
                if late(b, 2):
                    act.wait_ge(n_prod2, b - 1)
                nc.scalar.copy(slot_a[:, j, :], acc[:, 0, bass.ds(b * P, P)]).then_inc(n_slot2, 1)
            blocks2(act, sum_block)
            root(STEP_DEG, stat[:, 4, :])
            square(STEP_BN_CEN, 4)
            root(STEP_BN_VAR, chan[:, 1, :])
            square(STEP_CEN2, 6)
            root(STEP_VAR2, stat[:, 6, :])

            def fast1():
                def body(m, k):
                    for q in range(CT):
                        n = m * CT + q
                        act.wait_ge(c_counted, n + 1)
                        if q == 0 and late(m, 2):
                            act.wait_ge(c_product, m - 1)
                        nc.scalar.copy(adj[k][:, :, q, :], bank[q % 4][:, 0:KEYS].rearrange("p (b w) -> p b w", w=TW)
                                       ).then_inc(c_evac, 1)

                def part(n):
                    nc.scalar.copy(gcn_parts[:, n, :, :], h_rows[:, 0:HB, :]).then_inc(part_ready, 1)

                act.wait_ge(dve_step, STEP_T)
                part(0)
                body(0, 0)
                for n in range(1, PARTS):
                    act.wait_ge(rest_ready, n)
                    part(n)
                act.wait_ge(x1_stored, 16)
                units(act, body)

            with act.If(verdict == P):
                fast1()
            with act.Else():
                general_act(act, 1)
            act.wait_ge(edges_done[1], 1)
            def final_block(b, j):
                if late(b, 2):
                    act.wait_ge(f_prod, b - 1)
                nc.scalar.copy(slot_a[:, j, :], acc[:, 0, bass.ds(b * P, P)]).then_inc(f_slot, 1)
            blocks2(act, final_block)

        @block.vector
        def _(dve):
            steps = [0]

            def link(ins):
                steps[0] += 1
                ins.then_inc(dve_step, 1)
                dve.wait_ge(dve_step, steps[0])
                return steps[0]

            def rows_b(col):
                return col.unsqueeze(2).to_broadcast([P, NB, C])

            def cols_b(row):
                return row.unsqueeze(1).to_broadcast([P, NB, C])

            def layer_norm(cen, var, sq):
                link(nc.vector.tensor_reduce(stat[:, 0, :], x_rows[:, :, :], AX.X, ALU.add))
                link(nc.vector.tensor_scalar(stat[:, 1, :], stat[:, 0, :], 1.0 / C, None, ALU.mult))
                assert link(nc.vector.tensor_tensor(h_rows[:, :, :], x_rows[:, :, :], rows_b(stat[:, 1, :]),
                                                    ALU.subtract)) == cen
                dve.wait_ge(act_step, sq)
                link(nc.vector.tensor_reduce(stat[:, 0, :], scratch, AX.X, ALU.add))

            dve.wait_ge(x_in, 16)
            layer_norm(STEP_CEN, STEP_VAR, 1)
            assert link(nc.vector.tensor_scalar(stat[:, 2, :], stat[:, 0, :], 1.0 / C, EPS, ALU.mult, ALU.add)) == STEP_VAR
            dve.wait_ge(index_in, 64)
            link(nc.vector.tensor_copy(first_f[:, :], first_i[:, :]))
            link(nc.vector.tensor_tensor(dst_rel[:, :].rearrange("p (g t) -> p g t", t=TPG),
                                         dst_i.rearrange("p (g t) -> p g t", t=TPG),
                                         first_i[:, :].unsqueeze(2).to_broadcast([P, GA, TPG]), ALU.subtract))
            link(nc.vector.tensor_tensor(rel_t, dst_i, first_t[:, :], ALU.subtract))
            within = []
            for n, (r, width) in enumerate(((dst_rel[:, :], W), (rel_t, TW))):
                link(nc.vector.tensor_reduce(flags[:, 4 * n:4 * n + 1], r, AX.X, ALU.min))
                link(nc.vector.tensor_reduce(flags[:, 4 * n + 1:4 * n + 2], r, AX.X, ALU.max))
                link(nc.vector.tensor_scalar(flags[:, 4 * n + 2:4 * n + 3], flags[:, 4 * n:4 * n + 1], 0.0, None, ALU.is_ge))
                link(nc.vector.scalar_tensor_tensor(
                    out=flags[:, 4 * n + 3:4 * n + 4], in0=flags[:, 4 * n + 1:4 * n + 2], scalar=float(width - 1),
                    in1=flags[:, 4 * n + 2:4 * n + 3], op0=ALU.is_le, op1=ALU.mult))
                within.append(flags[:, 4 * n + 3:4 * n + 4])
            nc.vector.tensor_tensor(flag_c[:, 3:4], within[0], within[1], ALU.mult).then_inc(flag_ok, 1)
            link(nc.vector.tensor_scalar(whole, src_a, P - 1, None, ALU.bitwise_and))
            link(nc.vector.tensor_copy(low[:, :], whole))
            link(nc.vector.tensor_scalar(whole, src_a, P.bit_length() - 1, TW.bit_length() - 1,
                                         ALU.logical_shift_right, ALU.logical_shift_left))
            nc.vector.tensor_tensor(key[:, :], whole, rel_t, ALU.add).then_inc(keys_ready, 1)
            dve.wait_ge(flag_sum, 1)
            nc.vector.tensor_copy(flag_i[0:1, 0:1], bank[7][0:1, 0:1]).then_inc(flag_ready, 1)
            dve.wait_ge(act_step, 2)
            link(nc.vector.reciprocal(stat[:, 3, :], stat[:, 2, :]))
            assert link(nc.vector.scalar_tensor_tensor(out=h_rows[:, :, :], in0=h_rows[:, :, :], scalar=0.0,
                                                       in1=rows_b(stat[:, 3, :]), op0=ALU.max, op1=ALU.mult)) == STEP_H

            dve.wait_ge(weights_ready, 3 + 2 * SLOTS)
            def tables(b, j):
                dve.wait_ge(t_made, b + 1)
                if late(b, 2):
                    dve.wait_ge(t_stored[j], (b - j) * 16)
                nc.vector.tensor_tensor(slot_o[:, j, 0:2 * C], bank[2 + j][:, 0:2 * C], bias[:, :], ALU.add
                                        ).then_inc(t_dst, 1)
            blocks2(dve, tables)
            dve.wait_ge(acc_zero, 1)
            dve.wait_ge(keys_ready, 1)
            for j in range(2):
                dve.wait_ge(t_stored[j], 16 * NB)

            def one_hot(g, k, ready, used):
                if late(g, 2):
                    dve.wait_ge(used, g - 1)
                nc.vector.tensor_tensor(
                    hot[:, k, :, :], iota_w[:, :].unsqueeze(1).to_broadcast([P, TPG, W]),
                    dst_rel[:, bass.ds(g * TPG, TPG)].unsqueeze(2).to_broadcast([P, TPG, W]), ALU.is_equal
                ).then_inc(ready, 1)

            def accumulate(g, k, first, parts, ready, done):
                dve.wait_ge(ready, g + 1)
                if late(g, 1):
                    dve.wait_ge(done, g)
                place = acc[:, 0:parts, bass.ds(first, W)]
                nc.vector.tensor_tensor(place, bank[4 + k][:, 0:parts * W].rearrange("p (a w) -> p a w", a=parts),
                                        place, ALU.add).then_inc(done, 1)

            def fast0():
                def onehot_turned(g, s, i, first):
                    dve.wait_ge(edge_in[s], (i + 1) * 48)
                    nc.vector.tensor_scalar(lhs[D:P, s, :], dst_b[D:P, s, :], first_f[D:P, bass.ds(g, 1)],
                                            iota_p[D:P, :], ALU.subtract, ALU.is_equal).then_inc(onehot_t, 1)

                def add(g, s, i, _):
                    k = s % 2
                    dve.wait_ge(pre_b, g + 1)
                    dve.wait_ge(rows_in[s], (i + 1) * (16 * TPG))
                    if late(g, 2):
                        dve.wait_ge(fin, g - 1)
                    nc.vector.tensor_tensor(pre[:, k, :, :], bank[2 + k][:, :].rearrange("p (t c) -> p t c", t=2),
                                            got[:, s, 2:4, :], ALU.add).then_inc(added, 1)

                def finish(g, s, i, _):
                    k = s % 2
                    u, v = uv[:, k, :, 0:C], uv[:, k, :, C:2 * C]
                    dve.wait_ge(act_done, g + 1)
                    nc.vector.scalar_tensor_tensor(out=v[:, 0:2, :], in0=bank[k][:, :].rearrange("p (t c) -> p t c", t=2)[:, :, C:2 * C],
                                                   scalar=0.0, in1=v[:, 0:2, :], op0=ALU.max, op1=ALU.add).then_inc(val_a, 1)
                    nc.vector.scalar_tensor_tensor(out=v[:, 2:4, :], in0=pre[:, k, :, C:2 * C],
                                                   scalar=0.0, in1=v[:, 2:4, :], op0=ALU.max, op1=ALU.add).then_inc(val_a, 1)
                    one_hot(g, k, hot_ready, summed)
                    dve.wait_ge(val_a, (g + 1) * 2)
                    nc.vector.tensor_tensor(msg[:, k, :, :], v, u, ALU.mult).then_inc(fin, 1)

                def acc_stage(g, s, i, first):
                    accumulate(g, s % 2, first, 2, summed, accd)
                groups(dve, [(onehot_turned, 0), (add, 1), (finish, 2), (acc_stage, 3)], firsts(mybir.EngineType.DVE, 3))

            def fast1():
                def place(first, width):
                    return acc[:, 0, bass.ds(first, width)]

                def gathered_hot(m, a):
                    k = a % 2
                    if late(m, 1) or a >= 2:
                        dve.wait_ge(summed1, m * GATHERED + a - 1)
                    nc.vector.tensor_tensor(
                        hot[:, k, :, :], iota_w[:, :].unsqueeze(1).to_broadcast([P, TPG, W]),
                        dst_rel[:, bass.ds((m * UNIT + a) * TPG, TPG)].unsqueeze(2).to_broadcast([P, TPG, W]),
                        ALU.is_equal).then_inc(hot1_ready, 1)

                def gathered_add(n, k, first, counted):
                    dve.wait_ge(summed1, n + 1)
                    if late(n, 1):
                        dve.wait_ge(accd1, n)
                    if late(counted, 1):
                        dve.wait_ge(c_added, counted)
                    nc.vector.tensor_tensor(place(first, W), bank[4 + k][:, 0:W], place(first, W), ALU.add).then_inc(accd1, 1)

                def counted_hots(m, q):
                    n = m * CT + q
                    if late(n, 4):
                        dve.wait_ge(c_counted, n - 3)
                    t = (m * UNIT + GATHERED) * TPG + q
                    nc.vector.tensor_scalar(hot_k[:, q % 4, :], iota_k[:, :], key[:, bass.ds(t, 1)], None, ALU.is_equal
                                            ).then_inc(c_hot, 1)
                    nc.vector.tensor_scalar(hot_l[:, q % 4, :], iota_k[:, 0:P], low[:, bass.ds(t, 1)], None, ALU.is_equal
                                            ).then_inc(c_hot, 1)

                def counted_add(m, k, q, first, gathered):
                    n = m * CT + q
                    if q == 0:
                        dve.wait_ge(c_product, m + 1)
                    if late(n, 1):
                        dve.wait_ge(c_added, n)
                    dve.wait_ge(accd1, gathered)
                    nc.vector.tensor_tensor(place(first, TW), bank[6 + k][:, q * TW:(q + 1) * TW],
                                            place(first, TW), ALU.add).then_inc(c_added, 1)

                def body(m, k):
                    const = isinstance(m, int)
                    making, adding = not const or m < UNITS, not const or m >= 2
                    firsts_g = [None] * GATHERED
                    if not const or 1 <= m <= UNITS:
                        firsts_g[0], = first_dsts(first_i, (m - 1) * UNIT + GATHERED - 1, 1)
                    if making:
                        firsts_g[1:] = first_dsts(first_i, m * UNIT, GATHERED - 1)
                    if adding:
                        firsts_c = first_dsts(first_t, ((m - 2) * UNIT + GATHERED) * TPG, CT)
                    for q in range(CT):
                        if making:
                            counted_hots(m, q)
                        a, at = divmod(q, COUNTED)
                        if at == 0 and making:
                            gathered_hot(m, a)
                        if at == 2 and firsts_g[a] is not None and (making or (m == UNITS and a == 0)):
                            gathered_add(m * GATHERED + a - 1, (a - 1) % 2, firsts_g[a], (m - 2) * CT + q if adding else 0)
                        if adding:
                            done = m * GATHERED + (q + COUNTED - 2) // COUNTED - 1
                            if const:
                                done = min(done, UNITS * GATHERED)
                            counted_add(m - 2, k, q, firsts_c[q], done)

                body(0, 0)
                rest = h_rows[:, 0:HB, :]
                dve.wait_ge(gcn_stored, 16)
                for n in range(PARTS - 1):
                    dve.wait_ge(part_ready, n + 1)
                    nc.vector.tensor_tensor(rest, rest, gcn_parts[:, n, :, :], ALU.subtract).then_inc(rest_ready, 1)
                units(dve, body)
                body(UNITS, UNITS % 2)
                body(UNITS + 1, (UNITS + 1) % 2)

            def first_dsts(tile, at, n):
                _, regs = nc.values_load_multi_w_load_instructions(
                    tile[0:1, bass.ds(at, n)], engines=(mybir.EngineType.DVE,), min_val=0, max_val=N,
                    skip_runtime_bounds_check_because="a dst is a node, or N for the padding")
                return list(regs)

            verdict = sorted_enough(dve)
            with dve.If(verdict == P):
                fast0()
                dve.wait_ge(accd, G)
            with dve.Else():
                general_dve(dve, 0)
            nc.vector.memset(acc[:, :, N:NP], 0.0).then_inc(edges_done[0], 1)

            dve.wait_ge(n_prod, NB)
            link(nc.vector.tensor_copy(stat[:, 5, :], bank[6][:, 0:NB]))
            assert link(nc.vector.tensor_scalar(stat[:, 4, :], stat[:, 5, :], 1.0, None, ALU.max)) == STEP_DEG
            link(nc.vector.tensor_scalar(stat[:, 7, :], stat[:, 5, :], 1.0, None, ALU.max))
            link(nc.vector.reciprocal(stat[:, 2, :], stat[:, 7, :]))
            link(nc.vector.tensor_scalar(stat[:, 3, :], stat[:, 5, :], 1.0, None, ALU.min))
            def mean_block(b, j):
                dve.wait_ge(n_prod2, b + 1)
                rows = h_rows[:, bass.ds(b, 1), :].rearrange("p a c -> p (a c)")
                nc.vector.scalar_tensor_tensor(out=rows, in0=bank[j][:, 0:C], scalar=stat[:, 2, bass.ds(b, 1)],
                                               in1=rows, op0=ALU.mult, op1=ALU.add).then_inc(n_used2, 1)
            blocks2(dve, mean_block)
            dve.wait_ge(n_used2, NB)
            dve.wait_ge(act_step, 3)
            link(nc.vector.reciprocal(stat[:, 5, :], stat[:, 4, :]))
            link(nc.vector.tensor_tensor(stat[:, 4, :], stat[:, 5, :], stat[:, 3, :], ALU.mult))

            by_chan = h_rows[:, :, :].rearrange("p b c -> p c b")
            assert link(nc.vector.tensor_reduce(chan[:, 0, :], by_chan, AX.X, ALU.add)) == STEP_SUM
            dve.wait_ge(pe_step, 1)
            link(nc.vector.tensor_copy(chan[:, 1, :], bank[7][:, 0:C]))
            link(nc.vector.tensor_tensor(h_rows[:, :, :], h_rows[:, :, :], cols_b(chan[:, 1, :]), ALU.subtract))
            link(nc.vector.tensor_scalar(flag_c[:, 0:1], row_id[:, :], float(N % P), None, ALU.is_lt))
            link(nc.vector.tensor_scalar(h_rows[:, N // P, :], h_rows[:, N // P, :], flag_c[:, 0:1], None, ALU.mult))
            assert link(nc.vector.memset(h_rows[:, N // P + 1:NB, :], 0.0)) == STEP_BN_CEN
            dve.wait_ge(act_step, 4)
            assert link(nc.vector.tensor_reduce(chan[:, 0, :], scratch.rearrange("p b c -> p c b"), AX.X, ALU.add)) == STEP_SQ
            dve.wait_ge(pe_step, 2)
            assert link(nc.vector.tensor_scalar(chan[:, 1, :], bank[7][:, 0:C], EPS, None, ALU.add)) == STEP_BN_VAR
            dve.wait_ge(act_step, 5)
            link(nc.vector.reciprocal(chan[:, 2, :], chan[:, 1, :]))
            link(nc.vector.tensor_tensor(chan[:, 3, :], chan[:, 2, :], gamma_b[:, :], ALU.mult))
            link(nc.vector.tensor_tensor(h_rows[:, :, :], h_rows[:, :, :], cols_b(chan[:, 3, :]), ALU.mult))
            dve.wait_ge(beta_added, 1)
            link(nc.vector.tensor_tensor(x_rows[:, :, :], x_rows[:, :, :], h_rows[:, :, :], ALU.add))

            layer_norm(STEP_CEN2, STEP_VAR2, STEP_ACT_SQ2)
            assert link(nc.vector.tensor_scalar(stat[:, 6, :], stat[:, 0, :], 1.0 / C, EPS, ALU.mult, ALU.add)) == STEP_VAR2
            dve.wait_ge(act_step, STEP_ACT_SQ2 + 1)
            link(nc.vector.reciprocal(stat[:, 0, :], stat[:, 6, :]))
            link(nc.vector.tensor_tensor(stat[:, 1, :], stat[:, 0, :], stat[:, 4, :], ALU.mult))
            assert link(nc.vector.scalar_tensor_tensor(out=h_rows[:, :, :], in0=h_rows[:, :, :], scalar=0.0,
                                                       in1=rows_b(stat[:, 1, :]), op0=ALU.max, op1=ALU.mult)) == STEP_T

            dve.wait_ge(acc_zero1, 1)
            with dve.If(verdict == P):
                fast1()
                dve.wait_ge(accd1, UNITS * GATHERED)
                dve.wait_ge(c_added, UNITS * CT)
            with dve.Else():
                general_dve(dve, 1)
            nc.vector.memset(acc[:, 0, N:NP], 0.0).then_inc(edges_done[1], 1)

            def final_pair(b0):
                for j in range(2):
                    b = b0 + j
                    dve.wait_ge(f_prod, b + 1)
                    if late(b, 2):
                        dve.wait_ge(out_stored[j], b0 * 8)
                    nc.vector.scalar_tensor_tensor(out=slot_o[:, j, 0:C], in0=bank[j][:, 0:C], scalar=stat[:, 4, bass.ds(b, 1)],
                                                   in1=b1_b[:, :], op0=ALU.mult, op1=ALU.add).then_inc(f_bias, 1)
                for j in range(2):
                    b = b0 + j
                    dve.wait_ge(f_bias, b + 1)
                    dve.wait_ge(x1_in[j], b0 * 8 + 16)
                    nc.vector.scalar_tensor_tensor(out=slot_o[:, j, C:2 * C], in0=slot_o[:, j, 0:C], scalar=0.0,
                                                   in1=slot_o[:, j, 2 * C:3 * C],
                                                   op0=ALU.max, op1=ALU.add).then_inc(f_out, 1)
            final_pair(0)
            with dve.Fori(1, NB // 2) as i:
                final_pair(i * 2)

        @block.tensor
        def _(pe):
            pe.wait_ge(pool_consts, 12)
            pe.wait_ge(flag_ok, 1)
            nc.tensor.matmul(bank[7][0:1, 0:1], flag_c[:, 3:4], ones[:, :], start=True, stop=True).then_inc(flag_sum, 1)
            pe.wait_ge(weights_ready, 3 + 2 * SLOTS)

            def turn(b, j):
                pe.wait_ge(t_copied, b + 1)
                if late(b, 2):
                    pe.wait_ge(t_slot, b - 1)
                nc.tensor.transpose(bank[j][:, 0:C], slot_a[:, j, :], ident[:, :]).then_inc(t_turned, 1)
                pe.wait_ge(t_slot, b + 1)
                if late(b, 2):
                    pe.wait_ge(t_dst, b - 1)
                    pe.wait_ge(t_src, b - 1)
                nc.tensor.matmul(bank[2 + j][:, 0:2 * C], slot_b[:, j, :], w_nodes[:, 0:2 * C], start=True, stop=True)
                nc.tensor.matmul(bank[4 + j][:, 0:2 * C], slot_b[:, j, :], w_nodes[:, 2 * C:4 * C], start=True, stop=True
                                 ).then_inc(t_made, 1)
            blocks2(pe, turn)
            pe.wait_ge(t_dst, NB)
            pe.wait_ge(t_src, NB)

            def fast0():
                def products(g, s, i, _):
                    k = s % 2
                    pe.wait_ge(onehot_t, g + 1)
                    if late(g, 2):
                        pe.wait_ge(added, g - 1)
                    for t in (2, 3):
                        last = nc.tensor.matmul(bank[2 + k][:, (t - 2) * 256:(t - 1) * 256], lhs[:, s, t * P:(t + 1) * P],
                                                rhs[:, s, :], start=True, stop=True)
                    last.then_inc(pre_b, 1)
                    pe.wait_ge(rows_in[s], (i + 1) * (16 * TPG))
                    if late(g, 2):
                        pe.wait_ge(fin, g - 1)
                    for t in (0, 1):
                        place = bank[k][:, t * 256:(t + 1) * 256]
                        nc.tensor.matmul(place, lhs[:, s, t * P:(t + 1) * P], rhs[:, s, :], start=True, stop=False)
                        last = nc.tensor.matmul(place, ident[:, :], got[:, s, t, :], start=False, stop=True)
                    last.then_inc(pre_a, 1)

                def sums(g, s, i, _):
                    k = s % 2
                    pe.wait_ge(fin, g + 1)
                    if late(g, 2):
                        pe.wait_ge(accd, g - 1)
                    for t in range(TPG):
                        nc.tensor.matmul(bank[4 + k][:, 0:W], msg[:, k, t, :], hot[:, k, t, :],
                                         start=(t == 0), stop=(t == TPG - 1))
                    hot_bf = hot[:, k, :, :].bitcast(bf16).rearrange("p t (w h) -> p t w h", h=2)
                    for t in range(TPG):
                        last = nc.tensor.matmul(bank[4 + k][:, W:2 * W], ones_bf[:, :], hot_bf[:, t, :, 1],
                                                start=(t == 0), stop=(t == TPG - 1))
                    last.then_inc(summed, 1)
                groups(pe, [(products, 0), (sums, 2)])

            def fast1():
                def gathered_sums(m, a):
                    k = a % 2
                    pe.wait_ge(rows1_in[a], (m + 1) * (16 * TPG))
                    n = m * GATHERED + a
                    pe.wait_ge(hot1_ready, n + 1)
                    if late(n, 2):
                        pe.wait_ge(accd1, n - 1)
                    for t in range(TPG):
                        last = nc.tensor.matmul(bank[4 + k][:, 0:W], got[:, a, t, 0:C], hot[:, k, t, :],
                                                start=(t == 0), stop=(t == TPG - 1))
                    last.then_inc(summed1, 1)

                def count(m, q):
                    n = m * CT + q
                    pe.wait_ge(c_hot, (n + 1) * 2)
                    if late(n, 4):
                        pe.wait_ge(c_evac, n - 3)
                    nc.tensor.matmul(bank[q % 4][:, 0:KEYS], hot_l[:, q % 4, :], hot_k[:, q % 4, :],
                                     start=True, stop=True).then_inc(c_counted, 1)

                def product(m, k, blocks):
                    if 0 in blocks:
                        pe.wait_ge(c_evac, (m + 1) * CT)
                        pe.wait_ge(part_ready, PARTS)
                        if late(m, 2):
                            pe.wait_ge(c_added, (m - 1) * CT)
                    for b in blocks:
                        for n in range(PARTS):
                            last = nc.tensor.matmul(bank[6 + k][:, 0:CT * TW], gcn_parts[:, n, b, :],
                                                    adj[k][:, b, :, :].rearrange("p t w -> p (t w)"),
                                                    start=(b == 0 and n == 0), stop=(b == HB - 1 and n == PARTS - 1))
                    if HB - 1 in blocks:
                        last.then_inc(c_product, 1)

                def body(m, k):
                    const = isinstance(m, int)
                    making, multiplying = not const or m < UNITS, not const or m >= 1
                    for q in range(CT):
                        if making:
                            count(m, q)
                        if multiplying and q:
                            product(m - 1, 1 - k, range(HB * (q - 1) // (CT - 1), HB * q // (CT - 1)))
                        if making and q % COUNTED == COUNTED - 1:
                            gathered_sums(m, q // COUNTED)
                body(0, 0)
                units(pe, body)
                body(UNITS, UNITS % 2)

            verdict = sorted_enough(pe)
            with pe.If(verdict == P):
                fast0()
            with pe.Else():
                general_pe(pe, 0)

            pe.wait_ge(edges_done[0], 1)
            def count_block(b, j):
                pe.wait_ge(n_slot, b + 1)
                nc.tensor.matmul(bank[6][:, bass.ds(b, 1)], slot_b[:, j, :], avg[:, :], start=True, stop=True).then_inc(n_prod, 1)
            blocks2(pe, count_block)
            def sum_block(b, j):
                pe.wait_ge(n_slot2, b + 1)
                if late(b, 2):
                    pe.wait_ge(n_used2, b - 1)
                nc.tensor.transpose(bank[j][:, 0:C], slot_a[:, j, :], ident[:, :]).then_inc(n_prod2, 1)
            blocks2(pe, sum_block)
            for n, step in enumerate((STEP_SUM, STEP_SQ)):
                pe.wait_ge(dve_step, step)
                nc.tensor.matmul(bank[7][:, 0:C], inv_n[:, :], chan[:, 0, :], start=True, stop=True).then_inc(pe_step, 1)

            with pe.If(verdict == P):
                fast1()
            with pe.Else():
                general_pe(pe, 1)
            pe.wait_ge(edges_done[1], 1)
            def final_block(b, j):
                pe.wait_ge(f_slot, b + 1)
                if late(b, 2):
                    pe.wait_ge(f_bias, b - 1)
                nc.tensor.matmul(bank[j][:, 0:C], slot_a[:, j, :], w1_s[:, :], start=True, stop=True).then_inc(f_prod, 1)
            blocks2(pe, final_block)


_OUT = ("out_dram", (NP, C), "float32")


def kernel(**inputs):
    import numpy as np
    import concourse.bacc as bacc
    from concourse.bass_utils import run_bass_kernel_spmd

    a = {k: np.asarray(v) for k, v in inputs.items()}
    x = np.zeros((NP, C), a["x"].dtype)
    x[:N] = a["x"]
    src = np.zeros(GA * GE, a["src"].dtype)
    src[:E] = a["src"]
    dst = np.full(GA * GE, N, a["dst"].dtype)
    dst[:E] = a["dst"]
    edge = np.zeros((G * GE, D), a["edge_attr_64"].dtype)
    edge[:E] = a["edge_attr_64"]
    arrays = {
        "x": x,
        "src": src.reshape(GA, TPG, P).transpose(0, 2, 1),
        "dst_cols": dst.reshape(TA, P).T,
        "dst_row": dst.reshape(GA, GE),
        "dst_first": dst[::GE],
        "dst_first_t": dst[::P],
        "src_cols": src.reshape(TA, P).T,
        "edge_t": edge.reshape(G, GE, D).transpose(0, 2, 1),
        "wf_t": a["L0_gnn_W_f"].T,
        "ws_t": a["L0_gnn_W_s"].T,
        "bf": a["L0_gnn_b_f"],
        "bs": a["L0_gnn_b_s"],
        "gamma": a["L0_gnn_gamma"],
        "beta": a["L0_gnn_beta"],
        "w1": a["L1_gnn_W"],
        "b1": a["L1_gnn_b"],
    }
    arrays = {f"in_{k}": np.ascontiguousarray(v) for k, v in arrays.items()}
    nc = bacc.Bacc("TRN2", target_bir_lowering=False, num_devices=1)
    args = [nc.dram_tensor(k, v.shape, mybir.dt.from_np(v.dtype), kind="ExternalInput").ap() for k, v in arrays.items()]
    name, shape, dtype = _OUT
    out = nc.dram_tensor(name, shape, mybir.dt.from_np(np.dtype(dtype)), kind="ExternalOutput").ap()
    program(nc, *args, out)
    r = run_bass_kernel_spmd(nc, [arrays], core_ids=[0])
    return r.results[0][name][:N]
```

```python
import concourse.bass as bass
from concourse import mybir
from contextlib import ExitStack

N = 6250
C = 128
D = 64
E = 206250
P = 128
NB = 50
NP = NB * P
TPG = 4
GE = TPG * P
SLOTS = 4
G = -(-E // (GE * SLOTS)) * SLOTS
ITERS = G // SLOTS
TILES = G * TPG
W = 64
GATHERED = SLOTS
COUNTED = 5
UNIT = GATHERED + COUNTED
UNITS = -(-G // UNIT)
CT = COUNTED * TPG
TW = 8
HB = -(-N // P)
KEYS = HB * TW
PARTS = 3
GA = UNITS * UNIT
TA = GA * TPG
AW = C + 1
EPS = 1e-5
EXP_LN = "natural_log_exp_and_others"
UB = 10
CHUNKS = NB // UB
RING = 5


def program(nc, x, src, dst_cols, dst_row, dst_first, dst_first_t, src_cols, edge_t, wf_t, ws_t, bf, bs, gamma, beta, w1, b1, out):
    f32, i32, bf16, f16 = mybir.dt.float32, mybir.dt.int32, mybir.dt.bfloat16, mybir.dt.float16
    ALU, ACT, AX = mybir.AluOpType, mybir.ActivationFunctionType, mybir.AxisListType

    table_dst = nc.dram_tensor("table_dst", (NP, 2 * C), f32).ap()
    table_src = nc.dram_tensor("table_src", (NP, 2 * C), f32).ap()
    table_gcn = nc.dram_tensor("table_gcn", (NP, C), f32).ap()
    x1_rows = nc.dram_tensor("x1_rows", (NP, C), f32).ap()
    acc_rows = [nc.dram_tensor(f"acc_rows{i}", (NP, AW), f32).ap() for i in range(2)]

    x_v = x.rearrange("(b p) c -> p b c", p=P)
    x1_v = x1_rows.rearrange("(b p) c -> p b c", p=P)
    gcn_v = table_gcn.rearrange("(b p) c -> p b c", p=P)

    ctx = ExitStack()
    with ctx:
        def sb(name, shape, dt=f32):
            return ctx.enter_context(nc.sbuf_tensor(name, shape, dt))

        def sem(name):
            return ctx.enter_context(nc.semaphore(name))

        def sems(name, n):
            return [sem(f"{name}{i}") for i in range(n)]

        x_rows = sb("x_rows", [P, NB, C])
        h_rows = sb("h_rows", [P, NB, C])
        acc = sb("acc", [P, 2, NP])
        scratch = acc[:, 0, :].rearrange("p (b c) -> p b c", c=C)
        dst_rel = sb("dst_rel", [P, TA])
        first_i = sb("first_i", [P, GA], i32)
        first_f = sb("first_f", [P, GA])
        first_t = sb("first_t", [P, TA], i32)
        keys = sb("keys", [P, 2, TA], f16)
        keys_u = sb("keys_u", [P, 2, CT], f16)
        rel_u = sb("rel_u", [P, GATHERED, TPG])
        iota_k = sb("iota_k", [P, KEYS], f16)
        hot_k = sb("hot_k", [P, 4, KEYS], f16)
        hot_l = sb("hot_l", [P, 4, P], f16)
        ident = sb("ident", [P, P])
        iota_w = sb("iota_w", [P, W])
        iota_p = sb("iota_p", [P, 1])
        row_id = sb("row_id", [P, 1])
        ones_bf = sb("ones_bf", [P, P], bf16)
        inv_n = sb("inv_n", [P, P])
        avg = sb("avg", [P, 1])
        ones = sb("ones", [P, 1])
        below = sb("below", [P, P])
        w_nodes = sb("w_nodes", [P, 4 * C])
        w_edge = sb("w_edge", [D, 2 * C])
        bias = sb("bias", [P, 2 * C])
        gamma_b = sb("gamma_b", [P, C])
        beta_b = sb("beta_b", [P, C])
        w1_s = sb("w1_s", [P, C])
        b1_b = sb("b1_b", [P, C])
        stat = sb("stat", [P, 8, NB])
        chan = sb("chan", [P, 4, C])
        flag_c = sb("flag_c", [P, 4])
        flags = sb("flags", [P, 8])
        limits = sb("limits", [P, 2])
        flag_i = sb("flag_i", [1, 1], i32)
        slots = sb("slots", [P, RING, 2, C])
        src_i = sb("src_i", [P, SLOTS, TPG], i32)
        got = sb("got", [P, SLOTS, TPG, 2 * C])
        slot_o = got[:, :, :, :].rearrange("p s t c -> p (s t c)")[:, 0:RING * 4 * C].rearrange("p (r c) -> p r c", r=RING)
        rhs = sb("rhs", [P, SLOTS, 2 * C])
        hot = sb("hot", [P, 2, TPG, W])
        parts_words = PARTS * HB * C // 2
        ring = sb("ring", [P, max(parts_words, 2 * SLOTS * GE + SLOTS * 2 * C + 16 * C + 2 * TPG * C)])
        at = [0]

        def carve(words, dims, **sizes):
            at[0] += words
            return ring[:, at[0] - words:at[0]].rearrange(f"p ({dims}) -> p {dims}", **sizes)
        lhs = carve(SLOTS * GE, "s e", s=SLOTS)
        dst_b = carve(SLOTS * GE, "s e", s=SLOTS).bitcast(i32)
        pre = carve(8 * C, "k t c", k=2, t=2)
        uv = carve(4 * TPG * C, "k t c", k=2, t=TPG)
        msg = carve(2 * TPG * C, "k t c", k=2, t=TPG)
        dst_i, src_a, rel_t = (ring[:, n * TA:(n + 1) * TA] for n in range(3))
        dst_i, src_a = dst_i.bitcast(i32), src_a.bitcast(i32)
        whole = ring[:, 3 * TA:4 * TA].bitcast(i32)
        over = ring[:, 4 * TA:5 * TA]
        gcn_parts = ring[:, 0:parts_words].bitcast(bf16).rearrange("p (q b c) -> p q b c", q=PARTS, b=HB)
        adj = [words[:, 0:HB * CT * TW // 2].bitcast(f16).rearrange("p (b t w) -> p b t w", b=HB, t=CT)
               for words in (acc[:, 1, :], x_rows[:, :, :].rearrange("p b c -> p (b c)"))]
        bank = [ctx.enter_context(nc.psum_tensor(f"bank{i}", [P, 512], f32)) for i in range(8)]

        x_in = sems("x_in", CHUNKS)
        consts_in, index_in, pool_consts = sem("consts_in"), sem("index_in"), sem("pool_consts")
        weights_ready, flag_ok, flag_sum, flag_ready = sem("weights_ready"), sem("flag_ok"), sem("flag_sum"), sem("flag_ready")
        dve_step = sem("dve_step")
        ln_cen, ln_sq, ln_var, ln_root, ln_done = (sems(n, 2) for n in ("ln_cen", "ln_sq", "ln_var", "ln_root", "ln_done"))
        rel_ready, rel_consts, outside = sem("rel_ready"), sem("rel_consts"), sem("outside")
        deg_ready, deg_root, bn_sum, bn_cen, bn_sq, bn_sqsum, bn_var, bn_root, bn_scale, bn_scaled = (sem(n) for n in (
            "deg_ready", "deg_root", "bn_sum", "bn_cen", "bn_sq", "bn_sqsum", "bn_var", "bn_root", "bn_scale", "bn_scaled"))
        x1_back = sem("x1_back")
        acc_zero, acc_zero1 = sem("acc_zero"), sem("acc_zero1")
        t_copied, t_turned, t_slot, t_made, t_dst, t_src = (sem(n) for n in (
            "t_copied", "t_turned", "t_slot", "t_made", "t_dst", "t_src"))
        t_stored = sems("t_stored", RING)
        edge_in, srcs_in, rows_in = sems("edge_in", SLOTS), sems("srcs_in", SLOTS), sems("rows_in", SLOTS)
        onehot_t, pre_b, pre_a, added, act_done, fin, val_a, hot_ready, summed, accd = (sem(n) for n in (
            "onehot_t", "pre_b", "pre_a", "added", "act_done", "fin", "val_ready", "hot_ready", "summed", "accumulated"))
        act_chain = sem("act_chain")
        edges_done = sems("edges_done", 2)
        n_slot, n_turned, n_used, n_counts = sem("n_slot"), sem("n_turned"), sem("n_used"), sem("n_counts")
        gcn_stored = sem("gcn_stored")
        srcs1_in, rows1_in = sems("srcs1_in", SLOTS), sems("rows1_in", SLOTS)
        hot1_ready, summed1, accd1 = sem("hot1_ready"), sem("summed1"), sem("accumulated1")
        keys_ready, keys_in, x1_stored, part_ready, rest_ready = sem("keys_ready"), sem("keys_in"), sem("x1_stored"), sem("part_ready"), sem("rest_ready")
        c_hot, c_counted, c_evac, c_product, c_added = (sem(n) for n in (
            "c_hot", "c_counted", "c_evac", "c_product", "c_added"))
        f_slot, f_prod, f_bias, f_out = sem("f_slot"), sem("f_prod"), sem("f_bias"), sem("f_out")
        out_stored = sems("out_stored", RING)
        beta_added, waits_taken = sem("beta_added"), sem("waits_taken")
        g_in, g_rows, g_pre, g_half, g_add, g_actc, g_act, g_msg, g_sum, g_index, g_out, g_scat, g_dve, g_one = (
            sems(n, 2) for n in ("g_in", "g_rows", "g_pre", "g_half", "g_add", "g_actc", "g_act", "g_msg", "g_sum",
                                 "g_index", "g_out", "g_scat", "g_dve", "g_one"))
        g_back, g_turned, g_turn, g_zeroed = (sems(n, 2) for n in ("g_back", "g_turned", "g_turn", "g_zeroed"))

        block = ctx.enter_context(nc.Block())

        def blocks(eng, step):
            for j in range(UB):
                step(j, j, 0)
            with eng.Fori(1, CHUNKS) as i:
                for j in range(UB):
                    step(i * UB + j, j, i)

        def ring_turn(j, i):
            return i * (UB // RING) + j // RING

        def groups(eng, stages, before=None, iters=ITERS):
            def body(i):
                regs = before(i) if before else None
                for s in range(SLOTS):
                    for stage, lag in stages:
                        turn, at = (i, s - lag) if s >= lag else (i - 1, s - lag + SLOTS)
                        if isinstance(turn, int) and turn < 0:
                            continue
                        stage(turn * SLOTS + at, at, turn, regs and regs[s])
            body(0)
            with eng.Fori(1, iters) as i:
                body(i)
            most = max(lag for _, lag in stages)
            regs = before(iters) if before and most else None
            for d in range(most):
                for stage, lag in stages:
                    if d < lag:
                        g = iters * SLOTS + d - lag
                        stage(g, g % SLOTS, iters - 1, regs and regs[d])

        def firsts(engine, lag):
            def load(i):
                at = i * SLOTS - lag
                skip = max(0, -at) if isinstance(i, int) else 0
                n = min(SLOTS, G - at) if isinstance(i, int) else SLOTS
                _, regs = nc.values_load_multi_w_load_instructions(
                    first_i[0:1, bass.ds(at + skip, n - skip)], engines=(engine,), min_val=0, max_val=N,
                    skip_runtime_bounds_check_because="a dst is a node, or N for the padding")
                return [None] * skip + list(regs)
            return load

        def units(eng, body):
            assert UNITS % 2 == 1
            body(1, 1)
            body(2, 0)
            with eng.Fori(1, UNITS // 2) as i:
                body(i * 2 + 1, 1)
                body(i * 2 + 2, 0)

        def cols(n, c):
            return stat[:, n, c * UB:(c + 1) * UB]

        def chunk(rows, c):
            return rows[:, c * UB:(c + 1) * UB, :]

        def late(g, n):
            return not isinstance(g, int) or g >= n

        def take_waits(eng):
            eng.sem_inc(waits_taken, 1)

        def tables_stored(eng):
            for r in range(RING):
                eng.wait_ge(t_stored[r], 32 * (NB // RING))

        def sorted_enough(eng):
            eng.wait_ge(flag_ready, 1)
            return eng.value_load(flag_i[0:1, 0:1], min_val=0, max_val=P)

        def tiles(eng, step):
            for j in range(TPG):
                step(0, j, j)
            with eng.Fori(1, G) as g:
                for j in range(TPG):
                    step(g, j, g * TPG + j)

        g_same = hot[:, 0, :, :].rearrange("p t w -> p (t w)")[:, 0:P]
        g_before = hot[:, 1, :, :].rearrange("p t w -> p (t w)")[:, 0:P]
        g_msg_rows = uv[:, 1, 0, 0:AW]
        g_sum_rows = uv[:, 1, 1, 0:AW]
        g_uv = uv[:, 0, 0, :]
        g_col = flag_c
        g_dst, g_src, g_to = src_i[:, 1, 0:1], src_i[:, 0, 0:1], src_i[:, 2, 0:1]
        loads = (4, 3)

        def general_sync(sp, layer):
            sp.wait_ge(keys_ready, 1)
            sp.wait_ge((acc_zero, acc_zero1)[layer], 1)
            sp.dma_start(acc_rows[layer].rearrange("(b p) a -> p b a", p=P),
                         acc[:, 0, 0:AW].unsqueeze(1).to_broadcast([P, NB, AW])).then_inc(g_zeroed[layer], 16)
            sp.wait_ge(g_zeroed[layer], 16)

            def load(g, j, t):
                at = sp.snap(t) if not isinstance(t, int) else t
                if late(t, 1):
                    sp.wait_ge(g_scat[layer], t * 16)
                    take_waits(sp)
                sp.dma_start(g_src, src[bass.ds(g, 1), :, j:j + 1].rearrange("a p t -> (a p) t"),
                             allow_slow_non_contiguous=True).then_inc(g_in[layer], 16)
                sp.dma_start(g_dst, dst_cols[:, bass.ds(at, 1)], allow_slow_non_contiguous=True).then_inc(g_in[layer], 16)
                sp.dma_start(dst_b[:, 0, 0:P], dst_row[bass.ds(g, 1), j * P:(j + 1) * P].rearrange("a e -> (a e)")
                             .partition_broadcast(P)).then_inc(g_in[layer], 16)
                if layer == 0:
                    sp.dma_start(lhs[0:D, 0, 0:P], edge_t[bass.ds(g, 1), :, j * P:(j + 1) * P]
                                 .rearrange("a k e -> (a k) e")).then_inc(g_in[layer], 16)
            tiles(sp, load)
            sp.wait_ge(g_scat[layer], 16 * TILES)
            def back(b, j, i):
                rows = sp.snap(b * P) if not isinstance(b, int) else b * P
                if late(b, 1):
                    sp.wait_ge(g_turn[layer], b)
                take_waits(sp)
                sp.dma_start(slot_o[:, j % 2, 0:AW], acc_rows[layer][bass.ds(rows, P), :]).then_inc(g_back[layer], 16)
            blocks(sp, back)

        def general_pool(pool, layer):
            def move(g, j, t):
                pool.wait_ge(g_in[layer], (t + 1) * (16 * loads[layer]))
                take_waits(pool)
                if layer == 0:
                    pool.indirect_dma_start(out=got[:, 0, 0, :], out_offset=None, in_=table_dst,
                                            in_offset=bass.IndirectOffsetOnAxis(ap=g_dst, axis=0)).then_inc(g_rows[layer], 16)
                table, width = ((table_src, 2 * C), (table_gcn, C))[layer]
                pool.indirect_dma_start(out=got[:, 0, 1, 0:width], out_offset=None, in_=table,
                                        in_offset=bass.IndirectOffsetOnAxis(ap=g_src, axis=0)).then_inc(g_rows[layer], 16)
                pool.wait_ge(g_out[layer], t + 1)
                take_waits(pool)
                pool.indirect_dma_start(out=acc_rows[layer], out_offset=bass.IndirectOffsetOnAxis(ap=g_to, axis=0),
                                        in_=g_sum_rows, in_offset=None, compute_op=ALU.add).then_inc(g_scat[layer], 16)
            tiles(pool, move)

        def general_act(act, layer):
            if layer:
                return
            u, v = g_uv[:, 0:C], g_uv[:, C:2 * C]
            nc.scalar.preload_act_table_set(EXP_LN)
            def acts(g, j, t):
                act.wait_ge(g_add[0], t + 1)
                nc.scalar.activation(u, pre[:, 0, 1, 0:C], ACT.Exp).then_inc(g_actc[0], 1)
                nc.scalar.activation(v, pre[:, 0, 1, C:2 * C], ACT.Abs).then_inc(g_actc[0], 1)
                act.wait_ge(g_actc[0], t * 4 + 2)
                nc.scalar.activation(v, v, ACT.Exp, scale=-1.0).then_inc(g_actc[0], 1)
                act.wait_ge(g_actc[0], t * 4 + 3)
                nc.scalar.activation(g_uv, g_uv, ACT.Ln, bias=1.0).then_inc(g_actc[0], 1)
                act.wait_ge(g_actc[0], t * 4 + 4)
                nc.scalar.activation(u, u, ACT.Exp, scale=-1.0).then_inc(g_act[0], 1)
            tiles(act, acts)

        def general_dve(dve, layer):
            n_links = (7, 6)[layer]
            link_sem = g_dve[layer]
            nc.vector.memset(g_msg_rows[:, C:AW], 1.0).then_inc(g_one[layer], 1)
            nc.vector.tensor_scalar(g_col[:, 3:4], row_id[:, :], float(N + 1), None, ALU.add).then_inc(g_one[layer], 1)
            dve.wait_ge(g_one[layer], 2)

            def work(g, j, t):
                made = [0]

                def link(ins):
                    made[0] += 1
                    ins.then_inc(link_sem, 1)
                    dve.wait_ge(link_sem, t * n_links + made[0])

                dve.wait_ge(g_in[layer], (t + 1) * (16 * loads[layer]))
                link(nc.vector.tensor_copy(g_col[:, 0:1], g_dst))
                link(nc.vector.tensor_scalar(g_same, dst_b[:, 0, 0:P], g_col[:, 0:1], None, ALU.is_equal))
                link(nc.vector.tensor_tensor(g_before, g_same, below[:, :], ALU.mult))
                link(nc.vector.tensor_reduce(g_col[:, 1:2], g_before, AX.X, ALU.add))
                link(nc.vector.tensor_scalar(g_col[:, 2:3], g_col[:, 1:2], 0.0, None, ALU.is_equal))
                link(nc.vector.tensor_scalar(g_col[:, 1:2], g_col[:, 0:1], g_col[:, 3:4], g_col[:, 2:3],
                                             ALU.subtract, ALU.mult))
                nc.vector.tensor_tensor(g_to, g_col[:, 1:2], g_col[:, 3:4], ALU.add).then_inc(g_index[layer], 1)
                dve.wait_ge(g_rows[layer], (t + 1) * (32, 16)[layer])
                if layer == 0:
                    dve.wait_ge(g_pre[0], t + 1)
                    nc.vector.tensor_tensor(pre[:, 0, 0, :], bank[2][:, 0:2 * C], got[:, 0, 0, :], ALU.add
                                            ).then_inc(g_half[0], 1)
                    dve.wait_ge(g_half[0], t + 1)
                    nc.vector.tensor_tensor(pre[:, 0, 1, :], pre[:, 0, 0, :], got[:, 0, 1, :], ALU.add
                                            ).then_inc(g_add[0], 1)
                    dve.wait_ge(g_act[0], t + 1)
                    link(nc.vector.scalar_tensor_tensor(out=g_uv[:, C:2 * C], in0=pre[:, 0, 1, C:2 * C], scalar=0.0,
                                                        in1=g_uv[:, C:2 * C], op0=ALU.max, op1=ALU.add))
                    nc.vector.tensor_tensor(g_msg_rows[:, 0:C], g_uv[:, C:2 * C], g_uv[:, 0:C], ALU.mult
                                            ).then_inc(g_msg[0], 1)
                else:
                    nc.vector.tensor_copy(g_msg_rows[:, 0:C], got[:, 0, 1, 0:C]).then_inc(g_msg[1], 1)
                assert made[0] == n_links
                dve.wait_ge(g_sum[layer], t + 1)
                dve.wait_ge(g_index[layer], t + 1)
                nc.vector.tensor_copy(g_sum_rows, bank[4][:, 0:AW]).then_inc(g_out[layer], 1)
            tiles(dve, work)
            def back(b, j, i):
                dve.wait_ge(g_turned[layer], b + 1)
                nc.vector.tensor_copy(acc[:, :, bass.ds(b * P, P)], bank[j % 2][:, 0:2 * P].rearrange("p (a n) -> p a n", a=2)
                                      ).then_inc(g_turn[layer], 1)
            blocks(dve, back)
            dve.wait_ge(g_turn[layer], NB)

        def general_pe(pe, layer):
            def work(g, j, t):
                if layer == 0:
                    pe.wait_ge(g_in[0], (t + 1) * (16 * loads[0]))
                    nc.tensor.matmul(bank[2][:, 0:2 * C], lhs[0:D, 0, 0:P], rhs[0:D, 0, :], start=True, stop=True
                                     ).then_inc(g_pre[0], 1)
                pe.wait_ge(g_msg[layer], t + 1)
                nc.tensor.matmul(bank[4][:, 0:AW], g_same, g_msg_rows, start=True, stop=True).then_inc(g_sum[layer], 1)
            tiles(pe, work)
            def back(b, j, i):
                pe.wait_ge(g_back[layer], (b + 1) * 16)
                if late(b, 2):
                    pe.wait_ge(g_turn[layer], b - 1)
                nc.tensor.transpose(bank[j % 2][:, 0:P], slot_o[:, j % 2, 0:C], ident[:, :])
                nc.tensor.matmul(bank[j % 2][:, P:2 * P], slot_o[:, j % 2, C:AW].to_broadcast([P, P]), ident[:, :],
                                 start=True, stop=True).then_inc(g_turned[layer], 1)
            blocks(pe, back)

        @block.sync
        def _(sp):
            for c in range(CHUNKS):
                sp.dma_start(chunk(x_rows, c), x_v[:, c * UB:(c + 1) * UB, :]).then_inc(x_in[c], 16)
            sp.dma_start(dst_i, dst_cols).then_inc(index_in, 16)
            sp.dma_start(src_a, src_cols).then_inc(index_in, 16)
            sp.dma_start(first_i[:, :], dst_first.partition_broadcast(P)).then_inc(index_in, 16)
            sp.dma_start(first_t[:, :], dst_first_t.partition_broadcast(P)).then_inc(index_in, 16)
            for k, part in enumerate((wf_t[0:C], ws_t[0:C], wf_t[C:2 * C], ws_t[C:2 * C])):
                sp.dma_start(w_nodes[:, k * C:(k + 1) * C], part).then_inc(consts_in, 16)
            sp.dma_start(w_edge[:, 0:C], wf_t[2 * C:2 * C + D]).then_inc(consts_in, 16)
            sp.dma_start(w_edge[:, C:2 * C], ws_t[2 * C:2 * C + D]).then_inc(consts_in, 16)
            for tile, row in ((bias[:, 0:C], bf), (bias[:, C:2 * C], bs), (gamma_b[:, :], gamma),
                              (beta_b[:, :], beta), (b1_b[:, :], b1)):
                sp.dma_start(tile, row.partition_broadcast(P)).then_inc(consts_in, 16)
            sp.dma_start(w1_s[:, :], w1).then_inc(consts_in, 16)

            def store_tables(b, j, i):
                rows = sp.snap(b * P) if not isinstance(b, int) else b * P
                r = j % RING
                sp.wait_ge(t_dst, b + 1)
                sp.wait_ge(t_src, b + 1)
                sp.dma_start(table_dst[bass.ds(rows, P), :], slot_o[:, r, 0:2 * C]).then_inc(t_stored[r], 16)
                sp.dma_start(table_src[bass.ds(rows, P), :], slot_o[:, r, 2 * C:4 * C]).then_inc(t_stored[r], 16)
            blocks(sp, store_tables)
            tables_stored(sp)

            def fast0():
                sp.wait_ge(keys_ready, 1)
                def load_edges(g, s, i, first):
                    if late(g, SLOTS):
                        sp.wait_ge(pre_a, g - SLOTS + 1)
                    sp.dma_start(lhs[0:D, s, :], edge_t[bass.ds(g, 1)].rearrange("a k e -> (a k) e")).then_inc(edge_in[s], 16)
                    sp.dma_start(dst_b[D:P, s, :], dst_row[bass.ds(g, 1), :].rearrange("a e -> (a e)")
                                 .partition_broadcast(W)).then_inc(edge_in[s], 16)
                    sp.dma_start(rhs[D:P, s, :], table_dst[bass.ds(first, W), :]).then_inc(edge_in[s], 16)
                    if late(g, SLOTS):
                        sp.wait_ge(rows_in[s], i * (16 * TPG))
                    sp.dma_start(src_i[:, s, :], src[bass.ds(g, 1)].rearrange("a p t -> (a p) t")).then_inc(srcs_in[s], 16)
                groups(sp, [(load_edges, 0)], firsts(mybir.EngineType.SP, 0))

            def fast1():
                def load_srcs(g, s, i, _):
                    if late(g, SLOTS):
                        sp.wait_ge(rows1_in[s], i * (16 * TPG))
                    at = i * UNIT + s
                    sp.dma_start(src_i[:, s, :], src[bass.ds(at, 1)].rearrange("a p t -> (a p) t")).then_inc(srcs1_in[s], 16)
                groups(sp, [(load_srcs, 0)], iters=UNITS)

            verdict = sorted_enough(sp)
            with sp.If(verdict == P):
                fast0()
            with sp.Else():
                general_sync(sp, 0)
            for c in range(CHUNKS):
                sp.wait_ge(ln_done[1], c + 1)
                sp.dma_start(chunk(gcn_v, c), chunk(h_rows, c)).then_inc(gcn_stored, 16)
            for c in range(CHUNKS):
                sp.dma_start(chunk(x1_v, c), chunk(x_rows, c)).then_inc(x1_stored, 16)
            with sp.If(verdict == P):
                fast1()
                sp.wait_ge(c_product, UNITS - 1)
            with sp.Else():
                sp.wait_ge(gcn_stored, 16 * CHUNKS)
                general_sync(sp, 1)
            sp.wait_ge(x1_stored, 16 * CHUNKS)
            sp.dma_start(x_rows[:, :, :], x1_v).then_inc(x1_back, 16)

            def store_out(b, j, i):
                rows = sp.snap(b * P) if not isinstance(b, int) else b * P
                r = j % RING
                sp.wait_ge(f_out, b + 1)
                sp.dma_start(out[bass.ds(rows, P), :], slot_o[:, r, C:2 * C]).then_inc(out_stored[r], 16)
            blocks(sp, store_out)
            for r in range(RING):
                sp.wait_ge(out_stored[r], 16 * (NB // RING))

        @block.gpsimd
        def _(pool):
            nc.gpsimd.memset(ident[:, :], 0.0).then_inc(pool_consts, 1)
            nc.gpsimd.memset(below[:, :], 1.0).then_inc(pool_consts, 1)
            nc.gpsimd.memset(ones_bf[:, :], 1.0).then_inc(pool_consts, 1)
            nc.gpsimd.memset(inv_n[:, :], 1.0 / N).then_inc(pool_consts, 1)
            nc.gpsimd.memset(avg[:, :], 1.0 / P).then_inc(pool_consts, 1)
            nc.gpsimd.memset(ones[:, :], 1.0).then_inc(pool_consts, 1)
            nc.gpsimd.iota(iota_w[:, :], pattern=[[1, W]], base=0, channel_multiplier=0,
                           allow_small_or_imprecise_dtypes=True).then_inc(pool_consts, 1)
            nc.gpsimd.iota(iota_p[:, :], pattern=[[0, 1]], base=-(P - W), channel_multiplier=1,
                           allow_small_or_imprecise_dtypes=True).then_inc(pool_consts, 1)
            nc.gpsimd.iota(row_id[:, :], pattern=[[0, 1]], base=0, channel_multiplier=1,
                           allow_small_or_imprecise_dtypes=True).then_inc(pool_consts, 1)
            nc.gpsimd.iota(iota_k[:, :], pattern=[[1, KEYS]], base=0, channel_multiplier=0,
                           allow_small_or_imprecise_dtypes=True).then_inc(pool_consts, 1)
            pool.wait_ge(pool_consts, 10)
            nc.gpsimd.affine_select(out=ident[:, :], in_=ident[:, :], compare_op=ALU.not_equal, fill=1.0, base=0,
                                    pattern=[[-1, P]], channel_multiplier=1).then_inc(pool_consts, 1)
            nc.gpsimd.affine_select(out=below[:, :], in_=below[:, :], compare_op=ALU.is_gt, fill=0.0, base=0,
                                    pattern=[[-1, P]], channel_multiplier=1).then_inc(pool_consts, 1)

            def copy_h(b, j, i):
                if j == 0:
                    pool.wait_ge(ln_done[0], i + 1)
                if late(b, RING):
                    pool.wait_ge(t_turned, b - RING + 1)
                nc.gpsimd.tensor_copy(slots[:, j % RING, 0, :], h_rows[:, bass.ds(b, 1), :].rearrange("p a c -> p (a c)")
                                      ).then_inc(t_copied, 1)
            blocks(pool, copy_h)
            nc.gpsimd.memset(acc[:, :, :], 0.0).then_inc(acc_zero, 1)
            tables_stored(pool)

            def gathers(table, width, rows, srcs, used, iters):
                def gather(g, s, i, _):
                    pool.wait_ge(srcs[s], (i + 1) * 16)
                    if late(g, SLOTS):
                        for done in used:
                            pool.wait_ge(done, g - SLOTS + 1)
                    take_waits(pool)
                    for t in range(TPG):
                        pool.indirect_dma_start(
                            out=got[:, s, t, 0:width], out_offset=None, in_=table,
                            in_offset=bass.IndirectOffsetOnAxis(ap=src_i[:, s, t:t + 1], axis=0)).then_inc(rows[s], 16)
                groups(pool, [(gather, 0)], iters=iters)

            verdict = sorted_enough(pool)
            with pool.If(verdict == P):
                gathers(table_src, 2 * C, rows_in, srcs_in, (pre_a, added), ITERS)
            with pool.Else():
                general_pool(pool, 0)
            pool.wait_ge(edges_done[0], 1)
            pool.wait_ge(consts_in, 16 * 12)
            nc.gpsimd.tensor_tensor(x_rows[:, :, :], x_rows[:, :, :],
                                    beta_b[:, :].unsqueeze(1).to_broadcast([P, NB, C]), ALU.add).then_inc(beta_added, 1)
            pool.wait_ge(bn_scale, 1)
            for c in range(CHUNKS):
                nc.gpsimd.tensor_tensor(chunk(h_rows, c), chunk(h_rows, c),
                                        chan[:, 3, :].unsqueeze(1).to_broadcast([P, UB, C]), ALU.mult).then_inc(bn_scaled, 1)
            pool.wait_ge(ln_done[1], CHUNKS)
            nc.gpsimd.memset(acc[:, 0, :], 0.0).then_inc(acc_zero1, 1)
            pool.wait_ge(gcn_stored, 16 * CHUNKS)
            with pool.If(verdict == P):
                gathers(table_gcn, C, rows1_in, srcs1_in, (summed1,), UNITS)
            with pool.Else():
                general_pool(pool, 1)

        @block.scalar
        def _(act):
            act.wait_ge(consts_in, 16 * 12)
            for part in (w_nodes[:, 0:C], w_nodes[:, 2 * C:3 * C], bias[:, 0:C]):
                nc.scalar.mul(part, part, -1.0).then_inc(weights_ready, 1)
            for s in range(SLOTS):
                nc.scalar.mul(rhs[0:D, s, 0:C], w_edge[:, 0:C], -1.0).then_inc(weights_ready, 1)
                nc.scalar.copy(rhs[0:D, s, C:2 * C], w_edge[:, C:2 * C]).then_inc(weights_ready, 1)

            def layer_norm(n):
                for c in range(CHUNKS + 1):
                    if c < CHUNKS:
                        act.wait_ge(ln_cen[n], c + 1)
                        nc.scalar.activation(chunk(scratch, c), chunk(h_rows, c), ACT.Square).then_inc(ln_sq[n], 1)
                    if c >= 1:
                        act.wait_ge(ln_var[n], c)
                        nc.scalar.activation(cols(2, c - 1), cols(2, c - 1), ACT.Sqrt).then_inc(ln_root[n], 1)

            act.wait_ge(rel_ready, 1)
            nc.scalar.activation(over[:, :], dst_rel[:, :], ACT.Relu, scale=-1.0, accum_out=flags[:, 0:1]).then_inc(outside, 1)
            act.wait_ge(outside, 1)
            nc.scalar.activation(over[:, :], dst_rel[:, :], ACT.Relu, bias=limits[:, 0:1], accum_out=flags[:, 1:2]).then_inc(outside, 1)
            act.wait_ge(rel_ready, 2)
            act.wait_ge(outside, 2)
            nc.scalar.activation(over[:, :], rel_t, ACT.Relu, scale=-1.0, accum_out=flags[:, 2:3]).then_inc(outside, 1)
            act.wait_ge(outside, 3)
            nc.scalar.activation(over[:, :], rel_t, ACT.Relu, bias=limits[:, 1:2], accum_out=flags[:, 3:4]).then_inc(outside, 1)
            layer_norm(0)

            def tables(b, j, i):
                act.wait_ge(t_turned, b + 1)
                if late(b, RING):
                    act.wait_ge(t_made, b - RING + 1)
                nc.scalar.copy(slots[:, j % RING, 1, :], bank[j % 2][:, 0:C]).then_inc(t_slot, 1)
                if late(b, 1):
                    src_rows(b - 1, (j - 1) % UB, i - (j == 0))

            def src_rows(b, j, i):
                act.wait_ge(t_made, b + 1)
                if late(b, RING):
                    act.wait_ge(t_stored[j % RING], ring_turn(j, i) * 32)
                nc.scalar.copy(slot_o[:, j % RING, 2 * C:4 * C], bank[4 + j % 2][:, 0:2 * C]).then_inc(t_src, 1)
            blocks(act, tables)
            src_rows(NB - 1, UB - 1, CHUNKS - 1)

            def fast0():
                nc.scalar.preload_act_table_set(EXP_LN)
                def acts(g, s, i, _):
                    k = s % 2
                    u, v = uv[:, k, :, 0:C], uv[:, k, :, C:2 * C]
                    act.wait_ge(added, g + 1)
                    if late(g, 2):
                        act.wait_ge(fin, g - 1)
                    nc.scalar.activation(u[:, 2:4, :], pre[:, k, :, 0:C], ACT.Exp).then_inc(act_chain, 1)
                    nc.scalar.activation(v[:, 2:4, :], pre[:, k, :, C:2 * C], ACT.Abs).then_inc(act_chain, 1)
                    act.wait_ge(pre_a, g + 1)
                    pa = bank[k][:, :].rearrange("p (t c) -> p t c", t=2)
                    nc.scalar.activation(u[:, 0:2, :], pa[:, :, 0:C], ACT.Exp).then_inc(act_chain, 1)
                    nc.scalar.activation(v[:, 0:2, :], pa[:, :, C:2 * C], ACT.Abs).then_inc(act_chain, 1)
                    act.wait_ge(act_chain, g * 6 + 4)
                    nc.scalar.activation(v, v, ACT.Exp, scale=-1.0).then_inc(act_chain, 1)
                    act.wait_ge(act_chain, g * 6 + 5)
                    nc.scalar.activation(uv[:, k, :, :], uv[:, k, :, :], ACT.Ln, bias=1.0).then_inc(act_chain, 1)
                    act.wait_ge(act_chain, g * 6 + 6)
                    nc.scalar.activation(u, u, ACT.Exp, scale=-1.0).then_inc(act_done, 1)
                groups(act, [(acts, 0)])

            verdict = sorted_enough(act)
            with act.If(verdict == P):
                fast0()
            with act.Else():
                general_act(act, 0)

            act.wait_ge(edges_done[0], 1)
            nc.scalar.preload_act_table(ACT.Sqrt)
            def acc_block(b, j, i):
                if late(b, RING):
                    act.wait_ge(n_turned, b - RING + 1)
                nc.scalar.copy(slots[:, j % RING, :, :], acc[:, :, bass.ds(b * P, P)]).then_inc(n_slot, 1)
            blocks(act, acc_block)
            act.wait_ge(deg_ready, 1)
            nc.scalar.activation(stat[:, 4, :], stat[:, 4, :], ACT.Sqrt).then_inc(deg_root, 1)
            for c in range(CHUNKS):
                act.wait_ge(bn_cen, c + 1)
                nc.scalar.activation(chunk(scratch, c), chunk(h_rows, c), ACT.Square).then_inc(bn_sq, 1)
            act.wait_ge(bn_var, 1)
            nc.scalar.activation(chan[:, 1, :], chan[:, 1, :], ACT.Sqrt).then_inc(bn_root, 1)
            layer_norm(1)

            def fast1():
                def body(m, k):
                    for q in range(CT):
                        n = m * CT + q
                        act.wait_ge(c_counted, n + 1)
                        if q == 0 and late(m, 2):
                            act.wait_ge(c_product, m - 1)
                        nc.scalar.copy(adj[k][:, :, q, :], bank[q % 4][:, 0:KEYS].rearrange("p (b w) -> p b w", w=TW)
                                       ).then_inc(c_evac, 1)

                def part(n):
                    nc.scalar.copy(gcn_parts[:, n, :, :], h_rows[:, 0:HB, :]).then_inc(part_ready, 1)

                act.wait_ge(ln_done[1], CHUNKS)
                part(0)
                body(0, 0)
                for n in range(1, PARTS):
                    act.wait_ge(rest_ready, n)
                    part(n)
                act.wait_ge(x1_stored, 16 * CHUNKS)
                units(act, body)

            with act.If(verdict == P):
                fast1()
            with act.Else():
                general_act(act, 1)
            act.wait_ge(edges_done[1], 1)
            def final_block(b, j, i):
                if late(b, RING):
                    act.wait_ge(f_prod, b - RING + 1)
                nc.scalar.copy(slots[:, j % RING, 0, :], acc[:, 0, bass.ds(b * P, P)]).then_inc(f_slot, 1)
            blocks(act, final_block)

        @block.vector
        def _(dve):
            steps = [0]

            def link(ins):
                steps[0] += 1
                ins.then_inc(dve_step, 1)
                dve.wait_ge(dve_step, steps[0])
                return steps[0]

            def rows_b(col):
                return col.unsqueeze(2).to_broadcast([P, UB, C])

            def cols_b(row):
                return row.unsqueeze(1).to_broadcast([P, UB, C])

            def layer_norm(n, source, scale):
                def centre(c):
                    source(c)
                    link(nc.vector.tensor_reduce(cols(0, c), chunk(x_rows, c), AX.X, ALU.add))
                    link(nc.vector.tensor_scalar(cols(1, c), cols(0, c), 1.0 / C, None, ALU.mult))
                    nc.vector.tensor_tensor(chunk(h_rows, c), chunk(x_rows, c), rows_b(cols(1, c)), ALU.subtract
                                            ).then_inc(ln_cen[n], 1)

                def variance(c):
                    dve.wait_ge(ln_sq[n], c + 1)
                    link(nc.vector.tensor_reduce(cols(0, c), chunk(scratch, c), AX.X, ALU.add))
                    nc.vector.tensor_scalar(cols(2, c), cols(0, c), 1.0 / C, EPS, ALU.mult, ALU.add).then_inc(ln_var[n], 1)

                def finish(c):
                    dve.wait_ge(ln_root[n], c + 1)
                    link(nc.vector.reciprocal(cols(3, c), cols(2, c)))
                    by = scale(c)
                    nc.vector.scalar_tensor_tensor(out=chunk(h_rows, c), in0=chunk(h_rows, c), scalar=0.0,
                                                   in1=rows_b(by), op0=ALU.max, op1=ALU.mult).then_inc(ln_done[n], 1)
                for c in range(CHUNKS + 2):
                    for stage, lag in ((centre, 0), (variance, 1), (finish, 2)):
                        if lag <= c < CHUNKS + lag:
                            stage(c - lag)

            dve.wait_ge(index_in, 64)
            nc.vector.memset(limits[:, 0:1], -float(W - 1)).then_inc(rel_consts, 1)
            nc.vector.memset(limits[:, 1:2], -float(TW - 1)).then_inc(rel_consts, 1)
            dve.wait_ge(rel_consts, 2)
            nc.vector.tensor_tensor(dst_rel[:, :].rearrange("p (g t) -> p g t", t=TPG),
                                    dst_i.rearrange("p (g t) -> p g t", t=TPG),
                                    first_i[:, :].unsqueeze(2).to_broadcast([P, GA, TPG]), ALU.subtract).then_inc(rel_ready, 1)
            dve.wait_ge(rel_ready, 1)
            nc.vector.tensor_tensor(rel_t, dst_i, first_t[:, :], ALU.subtract).then_inc(rel_ready, 1)

            def load_x(c):
                dve.wait_ge(x_in[c], 16)
            layer_norm(0, load_x, lambda c: cols(3, c))

            link(nc.vector.tensor_copy(first_f[:, :], first_i[:, :]))
            link(nc.vector.tensor_scalar(whole, src_a, P - 1, None, ALU.bitwise_and))
            link(nc.vector.tensor_copy(keys[:, 1, :], whole))
            link(nc.vector.tensor_scalar(whole, src_a, P.bit_length() - 1, TW.bit_length() - 1,
                                         ALU.logical_shift_right, ALU.logical_shift_left))
            nc.vector.tensor_tensor(keys[:, 0, :], whole, rel_t, ALU.add).then_inc(keys_ready, 1)
            dve.wait_ge(outside, 4)
            link(nc.vector.tensor_reduce(flags[:, 4:5], flags[:, 0:4], AX.X, ALU.add))
            nc.vector.tensor_scalar(flag_c[:, 3:4], flags[:, 4:5], 0.0, None, ALU.is_equal).then_inc(flag_ok, 1)
            dve.wait_ge(flag_sum, 1)
            nc.vector.tensor_copy(flag_i[0:1, 0:1], bank[7][0:1, 0:1]).then_inc(flag_ready, 1)

            dve.wait_ge(weights_ready, 3 + 2 * SLOTS)
            def tables(b, j, i):
                dve.wait_ge(t_made, b + 1)
                if late(b, RING):
                    dve.wait_ge(t_stored[j % RING], ring_turn(j, i) * 32)
                nc.vector.tensor_tensor(slot_o[:, j % RING, 0:2 * C], bank[2 + j % 2][:, 0:2 * C], bias[:, :], ALU.add
                                        ).then_inc(t_dst, 1)
            blocks(dve, tables)
            dve.wait_ge(acc_zero, 1)
            dve.wait_ge(keys_ready, 1)
            tables_stored(dve)

            def one_hot(g, k, ready, used):
                if late(g, 2):
                    dve.wait_ge(used, g - 1)
                nc.vector.tensor_tensor(
                    hot[:, k, :, :], iota_w[:, :].unsqueeze(1).to_broadcast([P, TPG, W]),
                    dst_rel[:, bass.ds(g * TPG, TPG)].unsqueeze(2).to_broadcast([P, TPG, W]), ALU.is_equal
                ).then_inc(ready, 1)

            def accumulate(g, k, first, parts, ready, done):
                dve.wait_ge(ready, g + 1)
                if late(g, 1):
                    dve.wait_ge(done, g)
                place = acc[:, 0:parts, bass.ds(first, W)]
                nc.vector.tensor_tensor(place, bank[4 + k][:, 0:parts * W].rearrange("p (a w) -> p a w", a=parts),
                                        place, ALU.add).then_inc(done, 1)

            def fast0():
                def onehot_turned(g, s, i, first):
                    dve.wait_ge(edge_in[s], (i + 1) * 48)
                    nc.vector.tensor_scalar(lhs[D:P, s, :], dst_b[D:P, s, :], first_f[D:P, bass.ds(g, 1)],
                                            iota_p[D:P, :], ALU.subtract, ALU.is_equal).then_inc(onehot_t, 1)

                def add(g, s, i, _):
                    k = s % 2
                    dve.wait_ge(pre_b, g + 1)
                    dve.wait_ge(rows_in[s], (i + 1) * (16 * TPG))
                    if late(g, 2):
                        dve.wait_ge(fin, g - 1)
                    nc.vector.tensor_tensor(pre[:, k, :, :], bank[2 + k][:, :].rearrange("p (t c) -> p t c", t=2),
                                            got[:, s, 2:4, :], ALU.add).then_inc(added, 1)

                def finish(g, s, i, _):
                    k = s % 2
                    u, v = uv[:, k, :, 0:C], uv[:, k, :, C:2 * C]
                    dve.wait_ge(act_done, g + 1)
                    nc.vector.scalar_tensor_tensor(out=v[:, 0:2, :], in0=bank[k][:, :].rearrange("p (t c) -> p t c", t=2)[:, :, C:2 * C],
                                                   scalar=0.0, in1=v[:, 0:2, :], op0=ALU.max, op1=ALU.add).then_inc(val_a, 1)
                    nc.vector.scalar_tensor_tensor(out=v[:, 2:4, :], in0=pre[:, k, :, C:2 * C],
                                                   scalar=0.0, in1=v[:, 2:4, :], op0=ALU.max, op1=ALU.add).then_inc(val_a, 1)
                    one_hot(g, k, hot_ready, summed)
                    dve.wait_ge(val_a, (g + 1) * 2)
                    nc.vector.tensor_tensor(msg[:, k, :, :], v, u, ALU.mult).then_inc(fin, 1)

                def acc_stage(g, s, i, first):
                    accumulate(g, s % 2, first, 2, summed, accd)
                groups(dve, [(onehot_turned, 0), (add, 1), (finish, 2), (acc_stage, 3)], firsts(mybir.EngineType.DVE, 3))

            def fast1():
                def place(first, width):
                    return acc[:, 0, bass.ds(first, width)]

                def gathered_hot(m, a):
                    k = a % 2
                    if late(m, 1) or a >= 2:
                        dve.wait_ge(summed1, m * GATHERED + a - 1)
                    nc.vector.tensor_tensor(
                        hot[:, k, :, :], iota_w[:, :].unsqueeze(1).to_broadcast([P, TPG, W]),
                        rel_u[:, a, :].unsqueeze(2).to_broadcast([P, TPG, W]), ALU.is_equal).then_inc(hot1_ready, 1)

                def gathered_add(n, k, first, counted):
                    dve.wait_ge(summed1, n + 1)
                    if late(n, 1):
                        dve.wait_ge(accd1, n)
                    if late(counted, 1):
                        dve.wait_ge(c_added, counted)
                    nc.vector.tensor_tensor(place(first, W), bank[4 + k][:, 0:W], place(first, W), ALU.add).then_inc(accd1, 1)

                def unit_keys(m):
                    if late(m, 1):
                        dve.wait_ge(c_hot, m * CT * 2)
                        dve.wait_ge(hot1_ready, m * GATHERED)
                    t = m * UNIT * TPG
                    nc.vector.tensor_copy(rel_u[:, :, :].rearrange("p a t -> p (a t)"), dst_rel[:, bass.ds(t, GATHERED * TPG)]
                                          ).then_inc(keys_in, 1)
                    nc.vector.tensor_copy(keys_u[:, :, :], keys[:, :, bass.ds(t + GATHERED * TPG, CT)]).then_inc(keys_in, 1)

                def counted_hots(m, q):
                    n = m * CT + q
                    if late(n, 4) and q % 2 == 0:
                        dve.wait_ge(c_counted, n - 2)
                    nc.vector.tensor_scalar(hot_k[:, q % 4, :], iota_k[:, :], keys_u[:, 0, q:q + 1], None, ALU.is_equal
                                            ).then_inc(c_hot, 1)
                    nc.vector.tensor_scalar(hot_l[:, q % 4, :], iota_k[:, 0:P], keys_u[:, 1, q:q + 1], None, ALU.is_equal
                                            ).then_inc(c_hot, 1)

                def counted_add(m, k, q, first, gathered):
                    n = m * CT + q
                    if q == 0:
                        dve.wait_ge(c_product, m + 1)
                    if late(n, 1):
                        dve.wait_ge(c_added, n)
                    if gathered is not None:
                        dve.wait_ge(accd1, gathered)
                    nc.vector.tensor_tensor(place(first, TW), bank[6 + k][:, q * TW:(q + 1) * TW],
                                            place(first, TW), ALU.add).then_inc(c_added, 1)

                def body(m, k):
                    const = isinstance(m, int)
                    making, adding = not const or m < UNITS, not const or m >= 2
                    firsts_g = [None] * GATHERED
                    if making:
                        unit_keys(m)
                    if not const or 1 <= m <= UNITS:
                        firsts_g[0], = first_dsts(first_i, (m - 1) * UNIT + GATHERED - 1, 1)
                    if making:
                        firsts_g[1:] = first_dsts(first_i, m * UNIT, GATHERED - 1)
                    if adding:
                        firsts_c = first_dsts(first_t, ((m - 2) * UNIT + GATHERED) * TPG, CT)
                    if making:
                        dve.wait_ge(keys_in, (m + 1) * 2)
                    for q in range(CT):
                        if making:
                            counted_hots(m, q)
                        a, at = divmod(q, COUNTED)
                        if at == 0 and making:
                            gathered_hot(m, a)
                        if at == 2 and firsts_g[a] is not None and (making or (m == UNITS and a == 0)):
                            gathered_add(m * GATHERED + a - 1, (a - 1) % 2, firsts_g[a], (m - 2) * CT + q if adding else 0)
                        if adding:
                            done = None
                            if at == 2:
                                done = m * GATHERED + a
                                if const:
                                    done = min(done, UNITS * GATHERED)
                            counted_add(m - 2, k, q, firsts_c[q], done)

                body(0, 0)
                rest = h_rows[:, 0:HB, :]
                dve.wait_ge(gcn_stored, 16 * CHUNKS)
                for n in range(PARTS - 1):
                    dve.wait_ge(part_ready, n + 1)
                    nc.vector.tensor_tensor(rest, rest, gcn_parts[:, n, :, :], ALU.subtract).then_inc(rest_ready, 1)
                units(dve, body)
                body(UNITS, UNITS % 2)
                body(UNITS + 1, (UNITS + 1) % 2)

            def first_dsts(tile, at, n):
                _, regs = nc.values_load_multi_w_load_instructions(
                    tile[0:1, bass.ds(at, n)], engines=(mybir.EngineType.DVE,), min_val=0, max_val=N,
                    skip_runtime_bounds_check_because="a dst is a node, or N for the padding")
                return list(regs)

            verdict = sorted_enough(dve)
            with dve.If(verdict == P):
                fast0()
                dve.wait_ge(accd, G)
            with dve.Else():
                general_dve(dve, 0)
            nc.vector.memset(acc[:, :, N:NP], 0.0).then_inc(edges_done[0], 1)

            def mean_block(b, j, i):
                if j % RING == 0:
                    dve.wait_ge(n_turned, b + RING)
                    if late(b, 1):
                        dve.wait_ge(n_used, b)
                    counts = bank[5 + j // RING][:, 0:RING]
                    c0 = bass.ds(b, RING)
                    nc.vector.tensor_copy(stat[:, 5, c0], counts).then_inc(n_counts, 1)
                    nc.vector.tensor_scalar(stat[:, 4, c0], counts, 1.0, None, ALU.max).then_inc(n_counts, 1)
                    turn = ring_turn(j, i)
                    dve.wait_ge(n_counts, turn * 3 + 2)
                    nc.vector.reciprocal(stat[:, 6, c0], stat[:, 4, c0]).then_inc(n_counts, 1)
                    dve.wait_ge(n_counts, turn * 3 + 3)
                rows = h_rows[:, bass.ds(b, 1), :].rearrange("p a c -> p (a c)")
                nc.vector.scalar_tensor_tensor(out=rows, in0=bank[j % RING][:, 0:C], scalar=stat[:, 6, bass.ds(b, 1)],
                                               in1=rows, op0=ALU.mult, op1=ALU.add).then_inc(n_used, 1)
            blocks(dve, mean_block)
            nc.vector.tensor_scalar(stat[:, 7, :], stat[:, 5, :], 1.0, None, ALU.min).then_inc(deg_ready, 1)
            link(nc.vector.tensor_scalar(flag_c[:, 0:1], row_id[:, :], float(N % P), None, ALU.is_lt))

            dve.wait_ge(bn_sum, 1)
            link(nc.vector.tensor_copy(chan[:, 0, :], bank[7][:, 0:C]))
            for c in range(CHUNKS):
                centred = nc.vector.tensor_tensor(chunk(h_rows, c), chunk(h_rows, c), cols_b(chan[:, 0, :]), ALU.subtract)
                if c == CHUNKS - 1:
                    link(centred)
                    link(nc.vector.memset(h_rows[:, N // P + 1:NB, :], 0.0))
                    centred = nc.vector.tensor_scalar(h_rows[:, N // P, :], h_rows[:, N // P, :], flag_c[:, 0:1], None, ALU.mult)
                centred.then_inc(bn_cen, 1)
            dve.wait_ge(deg_root, 1)
            link(nc.vector.reciprocal(stat[:, 5, :], stat[:, 4, :]))
            link(nc.vector.tensor_tensor(stat[:, 4, :], stat[:, 5, :], stat[:, 7, :], ALU.mult))
            dve.wait_ge(bn_sqsum, 1)
            nc.vector.tensor_scalar(chan[:, 1, :], bank[7][:, 0:C], EPS, None, ALU.add).then_inc(bn_var, 1)
            dve.wait_ge(bn_root, 1)
            link(nc.vector.reciprocal(chan[:, 2, :], chan[:, 1, :]))
            nc.vector.tensor_tensor(chan[:, 3, :], chan[:, 2, :], gamma_b[:, :], ALU.mult).then_inc(bn_scale, 1)
            dve.wait_ge(beta_added, 1)

            def make_x1(c):
                dve.wait_ge(bn_scaled, c + 1)
                link(nc.vector.tensor_tensor(chunk(x_rows, c), chunk(x_rows, c), chunk(h_rows, c), ALU.add))

            def with_degree(c):
                link(nc.vector.tensor_tensor(cols(6, c), cols(3, c), cols(4, c), ALU.mult))
                return cols(6, c)
            layer_norm(1, make_x1, with_degree)

            dve.wait_ge(acc_zero1, 1)
            with dve.If(verdict == P):
                fast1()
                dve.wait_ge(accd1, UNITS * GATHERED)
                dve.wait_ge(c_added, UNITS * CT)
            with dve.Else():
                general_dve(dve, 1)
            nc.vector.memset(acc[:, 0, N:NP], 0.0).then_inc(edges_done[1], 1)

            dve.wait_ge(x1_back, 16)
            def final(b0, half, i):
                for r in range(RING):
                    b = b0 + r
                    dve.wait_ge(f_prod, b + 1)
                    if late(b, RING):
                        dve.wait_ge(out_stored[r], ring_turn(half * RING, i) * 16)
                    nc.vector.scalar_tensor_tensor(out=slot_o[:, r, 0:C], in0=bank[r][:, 0:C], scalar=stat[:, 4, bass.ds(b, 1)],
                                                   in1=b1_b[:, :], op0=ALU.mult, op1=ALU.add).then_inc(f_bias, 1)
                for r in range(RING):
                    b = b0 + r
                    dve.wait_ge(f_bias, b + 1)
                    nc.vector.scalar_tensor_tensor(out=slot_o[:, r, C:2 * C], in0=slot_o[:, r, 0:C], scalar=0.0,
                                                   in1=x_rows[:, bass.ds(b, 1), :].rearrange("p a c -> p (a c)"),
                                                   op0=ALU.max, op1=ALU.add).then_inc(f_out, 1)
            for half in range(2):
                final(half * RING, half, 0)
            with dve.Fori(1, CHUNKS) as i:
                for half in range(2):
                    final(i * UB + half * RING, half, i)

        @block.tensor
        def _(pe):
            pe.wait_ge(pool_consts, 12)
            pe.wait_ge(flag_ok, 1)
            nc.tensor.matmul(bank[7][0:1, 0:1], flag_c[:, 3:4], ones[:, :], start=True, stop=True).then_inc(flag_sum, 1)
            pe.wait_ge(weights_ready, 3 + 2 * SLOTS)

            def turn(b, j, i):
                pe.wait_ge(t_copied, b + 1)
                if late(b, 2):
                    pe.wait_ge(t_slot, b - 1)
                nc.tensor.transpose(bank[j % 2][:, 0:C], slots[:, j % RING, 0, :], ident[:, :]).then_inc(t_turned, 1)
                if late(b, 1):
                    make(b - 1, (j - 1) % UB)

            def make(b, j):
                pe.wait_ge(t_slot, b + 1)
                if late(b, 2):
                    pe.wait_ge(t_dst, b - 1)
                    pe.wait_ge(t_src, b - 1)
                turned = slots[:, j % RING, 1, :]
                nc.tensor.matmul(bank[2 + j % 2][:, 0:2 * C], turned, w_nodes[:, 0:2 * C], start=True, stop=True)
                nc.tensor.matmul(bank[4 + j % 2][:, 0:2 * C], turned, w_nodes[:, 2 * C:4 * C], start=True, stop=True
                                 ).then_inc(t_made, 1)
            blocks(pe, turn)
            make(NB - 1, UB - 1)
            pe.wait_ge(t_dst, NB)
            pe.wait_ge(t_src, NB)

            def fast0():
                def products(g, s, i, _):
                    k = s % 2
                    pe.wait_ge(onehot_t, g + 1)
                    if late(g, 2):
                        pe.wait_ge(added, g - 1)
                    for t in (2, 3):
                        last = nc.tensor.matmul(bank[2 + k][:, (t - 2) * 256:(t - 1) * 256], lhs[:, s, t * P:(t + 1) * P],
                                                rhs[:, s, :], start=True, stop=True)
                    last.then_inc(pre_b, 1)
                    pe.wait_ge(rows_in[s], (i + 1) * (16 * TPG))
                    if late(g, 2):
                        pe.wait_ge(fin, g - 1)
                    for t in (0, 1):
                        place = bank[k][:, t * 256:(t + 1) * 256]
                        nc.tensor.matmul(place, lhs[:, s, t * P:(t + 1) * P], rhs[:, s, :], start=True, stop=False)
                        last = nc.tensor.matmul(place, ident[:, :], got[:, s, t, :], start=False, stop=True)
                    last.then_inc(pre_a, 1)

                def sums(g, s, i, _):
                    k = s % 2
                    pe.wait_ge(fin, g + 1)
                    if late(g, 2):
                        pe.wait_ge(accd, g - 1)
                    for t in range(TPG):
                        nc.tensor.matmul(bank[4 + k][:, 0:W], msg[:, k, t, :], hot[:, k, t, :],
                                         start=(t == 0), stop=(t == TPG - 1))
                    hot_bf = hot[:, k, :, :].bitcast(bf16).rearrange("p t (w h) -> p t w h", h=2)
                    for t in range(TPG):
                        last = nc.tensor.matmul(bank[4 + k][:, W:2 * W], ones_bf[:, :], hot_bf[:, t, :, 1],
                                                start=(t == 0), stop=(t == TPG - 1))
                    last.then_inc(summed, 1)
                groups(pe, [(products, 0), (sums, 2)])

            def fast1():
                def gathered_sums(m, a):
                    k = a % 2
                    pe.wait_ge(rows1_in[a], (m + 1) * (16 * TPG))
                    n = m * GATHERED + a
                    pe.wait_ge(hot1_ready, n + 1)
                    if late(n, 2):
                        pe.wait_ge(accd1, n - 1)
                    for t in range(TPG):
                        last = nc.tensor.matmul(bank[4 + k][:, 0:W], got[:, a, t, 0:C], hot[:, k, t, :],
                                                start=(t == 0), stop=(t == TPG - 1))
                    last.then_inc(summed1, 1)

                def count(m, q):
                    n = m * CT + q
                    pe.wait_ge(c_hot, (n + 1) * 2)
                    if late(n, 4):
                        pe.wait_ge(c_evac, n - 3)
                    nc.tensor.matmul(bank[q % 4][:, 0:KEYS], hot_l[:, q % 4, :], hot_k[:, q % 4, :],
                                     start=True, stop=True).then_inc(c_counted, 1)

                def product(m, k, blocks):
                    if 0 in blocks:
                        pe.wait_ge(c_evac, (m + 1) * CT)
                        pe.wait_ge(part_ready, PARTS)
                        if late(m, 2):
                            pe.wait_ge(c_added, (m - 1) * CT)
                    for b in blocks:
                        for n in range(PARTS):
                            last = nc.tensor.matmul(bank[6 + k][:, 0:CT * TW], gcn_parts[:, n, b, :],
                                                    adj[k][:, b, :, :].rearrange("p t w -> p (t w)"),
                                                    start=(b == 0 and n == 0), stop=(b == HB - 1 and n == PARTS - 1))
                    if HB - 1 in blocks:
                        last.then_inc(c_product, 1)

                def body(m, k):
                    const = isinstance(m, int)
                    making, multiplying = not const or m < UNITS, not const or m >= 1
                    for q in range(CT):
                        if making:
                            count(m, q)
                        if multiplying:
                            product(m - 1, 1 - k, range(HB * q // CT, HB * (q + 1) // CT))
                        if making and q % COUNTED == COUNTED - 1:
                            gathered_sums(m, q // COUNTED)
                body(0, 0)
                units(pe, body)
                body(UNITS, UNITS % 2)

            verdict = sorted_enough(pe)
            with pe.If(verdict == P):
                fast0()
            with pe.Else():
                general_pe(pe, 0)

            pe.wait_ge(edges_done[0], 1)
            def turn_acc(b, j):
                pe.wait_ge(n_slot, b + 1)
                if late(b, RING):
                    pe.wait_ge(n_used, b - RING + 1)
                nc.tensor.transpose(bank[j % RING][:, 0:C], slots[:, j % RING, 0, :], ident[:, :])
                nc.tensor.matmul(bank[5 + j // RING][:, j % RING:j % RING + 1], slots[:, j % RING, 1, :], avg[:, :],
                                 start=True, stop=True).then_inc(n_turned, 1)

            def add_mean(b):
                pe.wait_ge(n_used, b + 1)
                last = nc.tensor.matmul(bank[7][:, 0:C], inv_n[:, :], h_rows[:, bass.ds(b, 1), :].rearrange("p a c -> p (a c)"),
                                        start=isinstance(b, int) and b == 0, stop=isinstance(b, int) and b == NB - 1,
                                        skip_group_check=True)
                if isinstance(b, int) and b == NB - 1:
                    last.then_inc(bn_sum, 1)

            def means(i):
                for half in range(2):
                    for r in range(RING):
                        turn_acc(i * UB + half * RING + r, half * RING + r)
                    for r in range(RING):
                        b = i * UB + (half - 1) * RING + r
                        if late(b, 0):
                            add_mean(b)
            means(0)
            with pe.Fori(1, CHUNKS) as i:
                means(i)
            for b in range(NB - RING, NB):
                add_mean(b)
            for b in range(NB):
                if b % UB == 0:
                    pe.wait_ge(bn_cen, 1)
                    pe.wait_ge(bn_sq, b // UB + 1)
                last = nc.tensor.matmul(bank[7][:, 0:C], inv_n[:, :], scratch[:, b, :], start=(b == 0), stop=(b == NB - 1))
            last.then_inc(bn_sqsum, 1)

            with pe.If(verdict == P):
                fast1()
            with pe.Else():
                general_pe(pe, 1)
            pe.wait_ge(edges_done[1], 1)
            def final_block(b, j, i):
                pe.wait_ge(f_slot, b + 1)
                if late(b, RING):
                    pe.wait_ge(f_bias, b - RING + 1)
                nc.tensor.matmul(bank[j % RING][:, 0:C], slots[:, j % RING, 0, :], w1_s[:, :], start=True, stop=True
                                 ).then_inc(f_prod, 1)
            blocks(pe, final_block)


_OUT = ("out_dram", (NP, C), "float32")


def kernel(**inputs):
    import numpy as np
    import concourse.bacc as bacc
    from concourse.bass_utils import run_bass_kernel_spmd

    a = {k: np.asarray(v) for k, v in inputs.items()}
    x = np.zeros((NP, C), a["x"].dtype)
    x[:N] = a["x"]
    src = np.zeros(GA * GE, a["src"].dtype)
    src[:E] = a["src"]
    dst = np.full(GA * GE, N, a["dst"].dtype)
    dst[:E] = a["dst"]
    edge = np.zeros((G * GE, D), a["edge_attr_64"].dtype)
    edge[:E] = a["edge_attr_64"]
    arrays = {
        "x": x,
        "src": src.reshape(GA, TPG, P).transpose(0, 2, 1),
        "dst_cols": dst.reshape(TA, P).T,
        "dst_row": dst.reshape(GA, GE),
        "dst_first": dst[::GE],
        "dst_first_t": dst[::P],
        "src_cols": src.reshape(TA, P).T,
        "edge_t": edge.reshape(G, GE, D).transpose(0, 2, 1),
        "wf_t": a["L0_gnn_W_f"].T,
        "ws_t": a["L0_gnn_W_s"].T,
        "bf": a["L0_gnn_b_f"],
        "bs": a["L0_gnn_b_s"],
        "gamma": a["L0_gnn_gamma"],
        "beta": a["L0_gnn_beta"],
        "w1": a["L1_gnn_W"],
        "b1": a["L1_gnn_b"],
    }
    arrays = {f"in_{k}": np.ascontiguousarray(v) for k, v in arrays.items()}
    nc = bacc.Bacc("TRN2", target_bir_lowering=False, num_devices=1)
    args = [nc.dram_tensor(k, v.shape, mybir.dt.from_np(v.dtype), kind="ExternalInput").ap() for k, v in arrays.items()]
    name, shape, dtype = _OUT
    out = nc.dram_tensor(name, shape, mybir.dt.from_np(np.dtype(dtype)), kind="ExternalOutput").ap()
    program(nc, *args, out)
    r = run_bass_kernel_spmd(nc, [arrays], core_ids=[0])
    return r.results[0][name][:N]
```
